# Optimizing a Trainium2 kernel written in Bass

```python
import numpy as np
import jax
import jax.numpy as jnp

def _softmax(x, axis=-1):
    return jax.nn.softmax(x, axis=axis)

def _gelu(x):
    return jax.nn.gelu(x, approximate=True)

def _silu(x):
    return jax.nn.silu(x)

def _sigmoid(x):
    return jax.nn.sigmoid(x)

def _layernorm(x, axis=-1, eps=1e-05):
    m = jnp.mean(x, axis=axis, keepdims=True)
    v = jnp.var(x, axis=axis, keepdims=True)
    return (x - m) / jnp.sqrt(v + eps)

def _scatter_add(tgt, idx, src, axis=0):
    return tgt.at[idx].add(src)

def _segment_sum(src, seg, n):
    return jax.ops.segment_sum(src, seg, n)
kernel_name = 'mk_recurrent_d1_jaxref_r2_1e5ea2'

def setup_inputs(seed: int=0):
    np.random.seed(seed)
    _w = jnp.asarray

    def _L0_attn_setup():
        import jax, jax.numpy as jnp
        import numpy as np
        _A = np.array([[1, 1, 1, 0, 1, 1, 1, 0, 0, 0, 1, 1], [1, 1, 0, 1, 1, 1, 0, 0, 0, 1, 1, 0], [1, 0, 1, 1, 1, 0, 0, 0, 1, 1, 0, 1], [0, 1, 1, 1, 0, 0, 0, 1, 1, 0, 1, 1], [0, 0, 0, 0, 1, 1, 1, 1, 1, 1, 1, 1], [1, 1, 1, 1, 0, 0, 0, 0, 0, 0, 0, 0], [0, 0, 0, 0, 1, 1, 1, 1, 0, 0, 0, 0], [1, 1, 0, 0, 1, 1, 0, 0, 1, 1, 0, 0], [1, 0, 1, 0, 1, 0, 1, 0, 1, 0, 1, 0], [0, 1, 0, 1, 0, 1, 0, 1, 0, 1, 0, 1], [1, 0, 0, 1, 1, 0, 0, 1, 1, 0, 0, 1], [0, 1, 1, 0, 0, 1, 1, 0, 0, 1, 1, 0]], dtype=np.float32)
        _H = jnp.asarray(np.concatenate([_A.T, np.eye(12, dtype=np.float32)], axis=1))

        def _fractal_dimension(x):
            s = x.reshape(-1)
            sn = (s - s.min()) / (s.max() - s.min() + 1e-10)
            counts = []
            for sc in (2, 4, 8, 16, 32):
                blk = sn[:sc * sc]
                counts.append(jnp.maximum(jnp.sum(blk > blk.mean()).astype(jnp.float32), 1.0))
            lx = jnp.log(jnp.array([2.0, 4.0, 8.0, 16.0, 32.0], dtype=jnp.float32))
            ly = jnp.log(jnp.stack(counts))
            n = jnp.float32(5.0)
            num = n * jnp.sum(lx * ly) - jnp.sum(lx) * jnp.sum(ly)
            den = n * jnp.sum(lx * lx) - jnp.sum(lx) ** 2
            return jnp.clip(-num / den, 1.0, 2.0)

        def _wave_filter(D, d):
            k = jnp.fft.fftfreq(d).astype(jnp.float32)
            ka = jnp.abs(k) + 1e-08
            omega = 1.0 + 0.2 * D
            a = 1.0 + 0.5 * D
            b = 0.1 * D
            real = jnp.sin(omega * D + a * ka)
            phase = omega * D - ka + b * ka ** 2
            return real * jnp.exp(1j * phase)

        def _golay_correct(bits):
            syn = (bits @ _H.T > 0.5).astype(jnp.float32)
            w = syn.sum(-1)
            _, idx = jax.lax.top_k(syn, 3)
            take = (jnp.arange(3)[None, :] < jnp.minimum(w, 3.0)[:, None]).astype(jnp.float32)
            pattern = (jax.nn.one_hot(idx, 24, dtype=jnp.float32) * take[..., None]).sum(axis=1)
            do_fix = ((w > 0) & (w <= 3))[:, None]
            return jnp.where(do_fix, jnp.mod(bits + pattern, 2.0), bits)
        key = jax.random.key(seed)
        k1, k2, k3 = jax.random.split(key, 3)
        B, S, E = (8, 1024, 512)
        x = jax.random.normal(k1, (B, S, E), dtype=jnp.float32)
        W_el = jax.random.normal(k2, (E, 24), dtype=jnp.float32) * 0.02
        b_el = jnp.zeros((24,), dtype=jnp.float32)
        W_le = jax.random.normal(k3, (24, E), dtype=jnp.float32) * 0.02
        b_le = jnp.zeros((E,), dtype=jnp.float32)
        return {'x': x, 'W_el': W_el, 'b_el': b_el, 'W_le': W_le, 'b_le': b_le}
    _L0_attn_in = _L0_attn_setup()

    def _L0_ffn_setup():
        import jax, jax.numpy as jnp
        import numpy as np
        K_TOP = 2
        key = jax.random.key(seed)
        k1, k2, k3 = jax.random.split(key, 3)
        B, S, H, E = (4, 1024, 512, 8)
        hidden_states = jax.random.normal(k1, (B, S, H), dtype=jnp.float32)
        router_w = jax.random.normal(k2, (E, H), dtype=jnp.float32) * 0.02
        expert_weights = jax.random.normal(k3, (E, H, H), dtype=jnp.float32) * 0.02
        return {'hidden_states': hidden_states, 'router_w': router_w, 'expert_weights': expert_weights}
    _L0_ffn_in = _L0_ffn_setup()
    _d = {'L0_attn_x': _L0_attn_in['x'], 'L0_attn_W_el': _L0_attn_in['W_el'], 'L0_attn_b_el': _L0_attn_in['b_el'], 'L0_attn_W_le': _L0_attn_in['W_le'], 'L0_attn_b_le': _L0_attn_in['b_le'], 'L0_ffn_router_w': _L0_ffn_in['router_w'], 'L0_ffn_expert_weights': _L0_ffn_in['expert_weights']}
    _x0 = _d['L0_attn_x']
    _d['L0_attn_x'] = jax.random.normal(jax.random.fold_in(jax.random.key(seed), 1), (16, 1024, 512), dtype=_x0.dtype)
    del _x0
    return _d

def reference(L0_attn_x, L0_attn_W_el, L0_attn_b_el, L0_attn_W_le, L0_attn_b_le, L0_ffn_router_w, L0_ffn_expert_weights):

    def _L0_attn_ref(x, W_el, b_el, W_le, b_le):
        import jax, jax.numpy as jnp
        import numpy as np
        _A = np.array([[1, 1, 1, 0, 1, 1, 1, 0, 0, 0, 1, 1], [1, 1, 0, 1, 1, 1, 0, 0, 0, 1, 1, 0], [1, 0, 1, 1, 1, 0, 0, 0, 1, 1, 0, 1], [0, 1, 1, 1, 0, 0, 0, 1, 1, 0, 1, 1], [0, 0, 0, 0, 1, 1, 1, 1, 1, 1, 1, 1], [1, 1, 1, 1, 0, 0, 0, 0, 0, 0, 0, 0], [0, 0, 0, 0, 1, 1, 1, 1, 0, 0, 0, 0], [1, 1, 0, 0, 1, 1, 0, 0, 1, 1, 0, 0], [1, 0, 1, 0, 1, 0, 1, 0, 1, 0, 1, 0], [0, 1, 0, 1, 0, 1, 0, 1, 0, 1, 0, 1], [1, 0, 0, 1, 1, 0, 0, 1, 1, 0, 0, 1], [0, 1, 1, 0, 0, 1, 1, 0, 0, 1, 1, 0]], dtype=np.float32)
        _H = jnp.asarray(np.concatenate([_A.T, np.eye(12, dtype=np.float32)], axis=1))

        def _fractal_dimension(x):
            s = x.reshape(-1)
            sn = (s - s.min()) / (s.max() - s.min() + 1e-10)
            counts = []
            for sc in (2, 4, 8, 16, 32):
                blk = sn[:sc * sc]
                counts.append(jnp.maximum(jnp.sum(blk > blk.mean()).astype(jnp.float32), 1.0))
            lx = jnp.log(jnp.array([2.0, 4.0, 8.0, 16.0, 32.0], dtype=jnp.float32))
            ly = jnp.log(jnp.stack(counts))
            n = jnp.float32(5.0)
            num = n * jnp.sum(lx * ly) - jnp.sum(lx) * jnp.sum(ly)
            den = n * jnp.sum(lx * lx) - jnp.sum(lx) ** 2
            return jnp.clip(-num / den, 1.0, 2.0)

        def _wave_filter(D, d):
            k = jnp.fft.fftfreq(d).astype(jnp.float32)
            ka = jnp.abs(k) + 1e-08
            omega = 1.0 + 0.2 * D
            a = 1.0 + 0.5 * D
            b = 0.1 * D
            real = jnp.sin(omega * D + a * ka)
            phase = omega * D - ka + b * ka ** 2
            return real * jnp.exp(1j * phase)

        def _golay_correct(bits):
            syn = (bits @ _H.T > 0.5).astype(jnp.float32)
            w = syn.sum(-1)
            _, idx = jax.lax.top_k(syn, 3)
            take = (jnp.arange(3)[None, :] < jnp.minimum(w, 3.0)[:, None]).astype(jnp.float32)
            pattern = (jax.nn.one_hot(idx, 24, dtype=jnp.float32) * take[..., None]).sum(axis=1)
            do_fix = ((w > 0) & (w <= 3))[:, None]
            return jnp.where(do_fix, jnp.mod(bits + pattern, 2.0), bits)
        B, S, E = x.shape
        D = _fractal_dimension(x)
        filt = _wave_filter(D, E)
        x1 = jnp.fft.ifft(jnp.fft.fft(x, axis=-1) * filt, axis=-1).real.astype(x.dtype)
        lat = x1 @ W_el + b_el
        bits = (jax.nn.sigmoid(lat) > 0.5).astype(jnp.float32).reshape(B * S, 24)
        corrected = _golay_correct(bits).reshape(B, S, 24)
        return x1 + corrected @ W_le + b_le

    def _L0_ffn_ref(hidden_states, router_w, expert_weights):
        import jax, jax.numpy as jnp
        import numpy as np
        K_TOP = 2
        B, S, H = hidden_states.shape
        x = hidden_states.reshape(-1, H)
        logits = x @ router_w.T
        probs = jax.nn.softmax(logits, axis=-1)
        topk_vals, topk_idx = jax.lax.top_k(probs, K_TOP)
        topk_w = topk_vals / (topk_vals.sum(-1, keepdims=True) + 1e-06)
        expert_out = jnp.einsum('nh,eho->eno', x, expert_weights)
        combined = jnp.take_along_axis(expert_out.transpose(1, 0, 2), topk_idx[:, :, None], axis=1)
        combined = combined.transpose(1, 0, 2)
        remap_bias = jnp.take_along_axis(probs, topk_idx, axis=1).T[:, :, None]
        weights = topk_w.T[:, :, None]
        out = ((combined + remap_bias) * weights).sum(axis=0)
        return out.reshape(B, S, H)
    x = L0_attn_x
    xn = _layernorm(x, axis=-1)
    s = _L0_attn_ref(xn, L0_attn_W_el, L0_attn_b_el, L0_attn_W_le, L0_attn_b_le)
    g = _silu(_L0_ffn_ref(xn, L0_ffn_router_w, L0_ffn_expert_weights))
    x = x + s * g
    return x

_drawn_inputs = setup_inputs


def setup_inputs(seed=0):
    import zlib

    import numpy as np

    out = dict(_drawn_inputs(seed))
    spreads = {'L0_attn_b_el': (0.0, 0.8), 'L0_attn_b_le': (0.0, 0.376)}
    factors = {'L0_attn_W_el': 5.346, 'L0_attn_W_le': 3.598}
    for name, (base, spread) in spreads.items():
        noise = np.random.default_rng([zlib.crc32(name.encode()), seed]).standard_normal(out[name].shape)
        drawn = base * np.exp(spread * noise) if base else spread * noise
        out[name] = jnp.asarray(drawn.astype(out[name].dtype))
    for name, factor in factors.items():
        out[name] = (out[name] * factor).astype(out[name].dtype)
    return out
```

```python
import math
from contextlib import ExitStack

import numpy as np
import concourse.bass as bass
from concourse import mybir

F32 = mybir.dt.float32
F16 = mybir.dt.float16
BF16 = mybir.dt.bfloat16
ALU = mybir.AluOpType
ACT = mybir.ActivationFunctionType
AXX = mybir.AxisListType.X
RMAX = bass.bass_isa.ReduceOp.max

P = 128
HALVES = 2
GOLAY_N, GOLAY_R = 24, 12
XS = 1024.0
CS = 16384.0
WS = 8192.0
EPS = 1e-5
INFO_W = 64
BLOCKS = (2, 4, 8, 16, 32)


def fourier_constants(E):
    H = E // 2
    n = np.arange(H)
    rows, freq, weight = [], [], []
    for odd in (0, 1):
        ks = np.arange(odd, H + 1, 2)
        for kind in (np.cos, np.sin):
            for k in ks:
                if kind is np.sin and k in (0, H):
                    continue
                rows.append(kind(2 * np.pi * ((k * n) % E) / E))
                freq.append(k / E)
                weight.append((1.0 if k in (0, H) else 2.0) / E)
    C = E // P
    table = np.asarray(rows).reshape(C, P, H).transpose(1, 0, 2).reshape(P, C * H)
    ka = np.float32(np.asarray(freq, np.float32) + np.float32(1e-8)).reshape(C, P).T
    w = np.asarray(weight).reshape(C, P).T
    lx = np.log(np.asarray(BLOCKS, np.float64))
    n = len(BLOCKS)
    slope = -(n * lx - lx.sum()) / (n * (lx * lx).sum() - lx.sum() ** 2)
    slope = np.broadcast_to(slope, (P, n))
    ramp = np.broadcast_to(8.0 - np.arange(8), (P, 8))
    return np.ascontiguousarray(np.concatenate([table, ka, w, slope, ramp], axis=1), dtype=np.float32)


def build(nc, x_in, W_el, b_el, W_le, b_le, router_w, experts, consts, out):
    B, S, E = x_in.shape
    NE = experts.shape[0]
    N = B * S
    T = N // P
    C = E // P
    H = E // 2
    CH = H // P
    GT = 4
    NG = T // GT
    U = 4
    NL = NE + GOLAY_N
    LH = 4

    x_rows = x_in.rearrange("b s e -> (b s) e")
    out_rows = out.rearrange("b s e -> (b s) e")
    x_tiles = x_rows.rearrange("(t p) e -> p t e", p=P)
    info_dram = nc.dram_tensor("token_info", (N, INFO_W), F32, kind="Internal").ap()

    ctx = ExitStack()
    with ctx:
        def sb(name, shape, dt=F32):
            return ctx.enter_context(nc.sbuf_tensor(name, shape, dt))

        def sem(name):
            return ctx.enter_context(nc.semaphore(name))

        w_hi = sb("w_hi", [P, NE, C, E], F16)
        w_lo = sb("w_lo", [P, NE, C, E], F16)
        arena = sb("arena", [P, 14336])
        xbuf = sb("xbuf", [P, U, GT, E])
        info = sb("info", [P, T, INFO_W])
        cst = sb("cst", [P, C * H + 2 * C + len(BLOCKS) + NE])
        c_hi = sb("c_hi", [P, 2, CH, H], F16)
        c_lo = sb("c_lo", [P, 2, CH, H], F16)
        wle3 = sb("wle3", [96, E], BF16)
        ident = sb("ident", [P, P])
        ident_b = sb("ident_b", [P, P], BF16)
        wcat = sb("wcat", [P, C, NL])
        avg = sb("avg", [P, P])
        amax = sb("amax", [P, NE])
        amax_all = sb("amax_all", [P, NE])
        wscale = sb("wscale", [P, NE])
        unscale = sb("unscale", [P, NE])
        bel = sb("bel", [P, GOLAY_N])
        rstd = sb("rstd", [P, T])
        mean = sb("mean", [P, T])
        small = sb("small", [P, 256])
        psum = ctx.enter_context(nc.psum_tensor("banks", [P, 8, 512], F32))

        tab = cst[:, 0:C * H].rearrange("p (c h) -> p c h", c=C)
        o = C * H
        ka, kw = cst[:, o:o + C], cst[:, o + C:o + 2 * C]
        o += 2 * C
        slope_c = cst[:, o:o + len(BLOCKS)]
        ramp = cst[:, o + len(BLOCKS):o + len(BLOCKS) + NE]

        raw = arena[:, 0:8192].rearrange("p (s c e) -> p s c e", s=LH, c=C)
        wpm = arena[:, 8192:12288].rearrange("p (s c e) -> p s c e", s=2, c=C)
        xb = xbuf[:, :, :, :].rearrange("p u t e -> p (u t e)")
        x01 = xb[:, 0:1024]
        junk = xb[:, 1024:2048]
        tabf = xb[:, 2048:3072].rearrange("p (c h) -> p c h", c=C)
        cf = xb[:, 3072:4096].rearrange("p (s k h) -> p s k h", s=2, k=CH)
        welraw = xb[:, 4096:4096 + C * GOLAY_N].rearrange("p (c n) -> p c n", c=C)
        welpm = xb[:, 4224:4224 + C * GOLAY_N].rearrange("p (c n) -> p c n", c=C)
        msb = xb[:, 4352:4352 + C * GOLAY_N].rearrange("p (c n) -> p c n", c=C)
        rtr = xb[0:NE, 4608:4608 + E]
        wle = xb[0:96, 5120:5120 + E]
        wlpm = xb[0:96, 5632:5632 + E]
        wlh = xb[0:96, 6144:6144 + E // 2].bitcast(BF16)
        wlr = xb[0:96, 6656:6656 + E]
        wlm = xb[0:96, 7168:7168 + E // 2].bitcast(BF16)
        lat = arena[:, 0:NL * T].rearrange("p (n t) -> p n t", n=NL)
        xn1 = arena[:, 4096:4096 + 2 * E].rearrange("p (s e) -> p s e", s=2)
        xnT1 = arena[:, 5120:5120 + 2 * E].rearrange("p (s e) -> p s e", s=2)
        st6 = arena[:, 6144:6144 + 2 * GT * 6].rearrange("p (s t k) -> p s t k", s=2, t=GT)
        mv1 = arena[:, 6208:6208 + 2 * GT * 2].rearrange("p (s t k) -> p s t k", s=2, t=GT)
        rt1 = arena[:, 6240:6240 + 2 * 4 * GT].rearrange("p (s k t) -> p s k t", s=2, k=4)

        def scr(i, n):
            return xb[:, i:i + n * T].rearrange("p (n t) -> p n t", n=n)
        eq, sc, oh1, oh2, l2, ex = (scr(1024 * i, NE) for i in range(6))
        (m1, m2, mx1, mx2, zs, d2, e2, p1, p2, den, w1, w2, cc, nlow, nhigh, fix) = (
            xb[:, 6144 + T * i:6144 + T * (i + 1)] for i in range(16))
        bits = arena[:, 6400:6400 + GOLAY_N * T].rearrange("p (n t) -> p n t", n=GOLAY_N)
        fixadd = arena[:, 9472:9472 + GOLAY_R * T].rearrange("p (n t) -> p n t", n=GOLAY_R)
        we = arena[:, 11008:11008 + NE * T].rearrange("p (n t) -> p n t", n=NE)
        info_bits = info[:, :, 16:64].bitcast(BF16).rearrange("p t (g c) -> p t g c", g=3)

        x2 = xb[:, 0:U * E].rearrange("p (s e) -> p s e", s=U)
        def two(i):
            return xb[:, i:i + 2 * E].rearrange("p (s e) -> p s e", s=2)
        uv2, raw2, o2, ysb2, s2, sg2 = (two(U * E + 1024 * i) for i in range(6))
        def atwo(i):
            return arena[:, i:i + 2 * E].rearrange("p (s e) -> p s e", s=2)
        z2, g2 = atwo(0), atwo(1024)
        hi2 = arena[:, 2048:2048 + E].bitcast(F16).rearrange("p (s c e) -> p s c e", s=2, c=C)
        lo2 = arena[:, 2560:2560 + E].bitcast(F16).rearrange("p (s c e) -> p s c e", s=2, c=C)
        bT2 = arena[0:96, 3072:3072 + P].bitcast(BF16).rearrange("p (s e) -> p s e", s=2)
        inf2 = arena[:, 3328:3328 + U * INFO_W].rearrange("p (s w) -> p s w", s=U)

        v, at = {}, 0
        for name, m in (("st", 12), ("mv", 4), ("ve", 2), ("sd", 2), ("r0", 2), ("rt", 2), ("mu", 5), ("cnt", 5), ("ly", 5),
                        ("D", 1), ("wD", 1), ("a", 1), ("b", 1), ("arg", C), ("ph", C), ("s1", C), ("q1", C), ("q2", C)):
            v[name] = small[:, at:at + m]
            at += m
        v["st"] = v["st"].rearrange("p (r k) -> p r k", r=2)
        v["mv"] = v["mv"].rearrange("p (r k) -> p r k", r=2)

        c_lo_ready = sem("c_lo_ready")
        wcat_raw = sem("wcat_raw")
        wmean_mm = sem("wmean_mm")
        ones_ready = sem("ones_ready")
        ld_x01, ld_cst, ld_small, ld_router = sem("ld_x01"), sem("ld_cst"), sem("ld_small"), sem("ld_router")
        ld_w = [sem(f"ld_w{i}") for i in range(LH)]
        ld_x = [sem(f"ld_x{i}") for i in range(U)]
        dch = sem("vector_chain")
        ach = sem("scalar_chain")
        pch = sem("pool_chain")
        ident_ready = sem("ident_ready")
        d_ready = sem("d_ready")
        act_setup = sem("act_setup")
        filt_ready = sem("filt_ready")
        c_mm = sem("c_mm")
        c_copied = sem("c_copied")
        m_mm = sem("m_mm")
        wel_ready = sem("wel_ready")
        m_copied = sem("m_copied")
        wcat_ready = sem("wcat_ready")
        rt_mm = sem("rt_mm")
        amax_ready = sem("amax_ready")
        amax_red = sem("amax_red")
        wscale_ready = sem("wscale_ready")
        wpm_ready = sem("wpm_ready")
        whi_ready = sem("whi_ready")
        wlo_ready = sem("wlo_ready")
        wle_ready = sem("wle_ready")
        var_ready = sem("var_ready")
        sd_ready = sem("sd_ready")
        rstd_ready = sem("rstd_ready")
        xn_ready = sem("xn_ready")
        t1_done = sem("t1_done")
        t1_copied = sem("t1_copied")
        l_done = sem("l_done")
        lat_copied = sem("lat_copied")
        dx_ready = sem("dx_ready")
        exp_ready = sem("exp_ready")
        corr_ready = sem("corr_ready")
        info_ready = sem("info_ready")
        info_init = sem("info_init")
        info_stored = sem("info_stored")
        ld_x2 = [sem(f"ld_x2_{i}") for i in range(U)]
        uv_ready = sem("uv_ready")
        uvT_done = sem("uvT_done")
        hi_ready = sem("hi_ready")
        lo_ready = sem("lo_ready")
        e_done = sem("e_done")
        e_used = sem("e_used")
        y_done = sem("y_done")
        y_copied = sem("y_copied")
        z_ready = sem("z_ready")
        g_ready = sem("g_ready")
        s_ready = sem("s_ready")
        sg_ready = sem("sg_ready")
        raw_ready = sem("raw_ready")
        stats_ready = sem("stats_ready")
        aggr_ready = sem("aggr_ready")
        newton = sem("newton")
        mm1_done = sem("mm1_done")
        o_ready = sem("o_ready")
        stored = [sem(f"stored{i}") for i in range(2)]

        block = ctx.enter_context(nc.Block())

        def after(eng, s, v):
            if isinstance(v, int) and v <= 0:
                return
            eng.wait_ge(s, v)

        def rounds(eng, count, step):
            for k in range(U):
                step(0, k)
            with eng.Fori(1, count - 1) as i:
                for k in range(U):
                    step(i, k)
            for k in range(U):
                step(count - 1, k, last=True)

        @block.sync
        def _(sp):
            sp.dma_start(x01, x_rows[0:2, :].rearrange("n e -> (n e)").partition_broadcast(P)).then_inc(ld_x01, 16)
            sp.dma_start(cst[:, :], consts).then_inc(ld_cst, 16)
            sp.dma_start(welraw, W_el.rearrange("(c p) n -> p c n", p=P)).then_inc(ld_small, 16)
            sp.dma_start(bel[:, :], b_el.partition_broadcast(P)).then_inc(ld_small, 16)
            sp.wait_ge(info_init, 1)
            for g in range(3):
                sp.dma_start(wle[32 * g:32 * g + GOLAY_N, :], W_le).then_inc(ld_small, 16)
                sp.dma_start(wle[32 * g + GOLAY_N:32 * g + GOLAY_N + 1, :], b_le.rearrange("(a e) -> a e", a=1)).then_inc(ld_small, 16)
            sp.dma_start(rtr, router_w).then_inc(ld_router, 16)
            for e in range(NE):
                if e >= LH:
                    sp.wait_ge(wpm_ready, e - LH + 1)
                sp.dma_start(raw[:, e % LH], experts[e].rearrange("(c p) o -> p c o", p=P)).then_inc(ld_w[e % LH], 16)
            sp.wait_ge(wcat_ready, 1)
            sp.wait_ge(wle_ready, 1)

            def load(i, k):
                after(sp, t1_done, GT * ((i - 1) * U + k + 1))
                after(sp, aggr_ready, (i - 1) * U + k + 1)
                sp.dma_start(xbuf[:, k], x_tiles[:, bass.ds((i * U + k) * GT, GT), :]).then_inc(ld_x[k], 16)
            for k in range(U):
                load(0, k)
            with sp.Fori(1, NG // U) as i:
                for k in range(U):
                    load(i, k)
            sp.wait_ge(info_ready, 1)
            sp.dma_start(info_dram.rearrange("(t p) w -> p t w", p=P), info[:, :, :]).then_inc(info_stored, 16)
            sp.wait_ge(info_stored, 16)

            def load2(i, k):
                j = i * U + k
                after(sp, o_ready, j - U + 1)
                sp.dma_start(x2[:, k], x_rows[bass.ds(j * P, P), :]).then_inc(ld_x2[k], 16)
                sp.dma_start(inf2[:, k], info_dram[bass.ds(j * P, P), :]).then_inc(ld_x2[k], 16)

            def step(i, k, last=False):
                if not (last and k + U - 1 >= U):
                    load2(i + (k + U - 1) // U, (k + U - 1) % U)
                sp.wait_ge(o_ready, i * U + k + 1)
                sp.dma_start(out_rows[bass.ds((i * U + k) * P, P), :], o2[:, k % 2]).then_inc(stored[k % 2], 16)
            for k in range(U - 1):
                load2(0, k)
            rounds(sp, T // U, step)
            for b in range(2):
                sp.wait_ge(stored[b], 16 * (T // 2))

        @block.gpsimd
        def _(pool):
            n = [0]

            def link(ins):
                n[0] += 1
                ins.then_inc(pch, 1)
                pool.wait_ge(pch, n[0])
            link(nc.gpsimd.memset(wle, 0.0))
            nc.gpsimd.memset(info[:, :, :], 0.0).then_inc(info_init, 1)
            nc.gpsimd.memset(avg[:, :], 1.0 / E).then_inc(ones_ready, 1)
            link(nc.gpsimd.memset(ident[:, :], 0.0))
            nc.gpsimd.affine_select(out=ident[:, :], in_=ident[:, :], compare_op=ALU.not_equal, fill=1.0, base=0,
                                    pattern=[[-1, P]], channel_multiplier=1).then_inc(ident_ready, 1)
            pool.wait_ge(ident_ready, 1)
            nc.gpsimd.tensor_copy(ident_b[:, :], ident[:, :]).then_inc(ident_ready, 1)
            pool.wait_ge(info_init, 1)
            nc.gpsimd.memset(info_bits[:, :, :, GOLAY_N:GOLAY_N + 1], 1.0).then_inc(info_init, 1)
            for half in range(NE // LH):
                pool.wait_ge(amax_ready, LH * (half + 1))
                hs = slice(LH * half, LH * half + LH)
                nc.gpsimd.partition_all_reduce(amax_all[:, hs], amax[:, hs], P, RMAX).then_inc(amax_red, 1)
                for e in range(LH * half, LH * half + LH):
                    after(pool, whi_ready, e - 1)
                    after(pool, wlo_ready, e - 1)
                    r, w = raw[:, e % LH], wpm[:, e % 2]
                    nc.gpsimd.tensor_tensor(w[:, 0:CH], r[:, 0:CH], r[:, CH:C], ALU.add)
                    nc.gpsimd.tensor_tensor(w[:, CH:C], r[:, 0:CH], r[:, CH:C], ALU.subtract).then_inc(wpm_ready, 1)

            pool.wait_ge(wlo_ready, NE)
            pool.wait_ge(whi_ready, NE)

            pool.wait_ge(corr_ready, 1)
            pool.wait_ge(info_init, 2)
            for g in range(3):
                ins = nc.gpsimd.tensor_copy(info_bits[:, :, g, 0:GOLAY_N], bits.rearrange("p n t -> p t n"))
            ins.then_inc(corr_ready, 1)

            def prep(i, k):
                j, b = i * U + k, k % 2
                pool.wait_ge(ld_x2[k], 32 * (i + 1))
                after(pool, uv_ready, j - 1)
                nc.gpsimd.tensor_tensor(raw2[:, b, 0:H], x2[:, k, 0:H], x2[:, k, H:E], ALU.add)
                nc.gpsimd.tensor_tensor(raw2[:, b, H:E], x2[:, k, 0:H], x2[:, k, H:E], ALU.subtract).then_inc(raw_ready, 1)

            def step(i, k, last=False):
                j, b = i * U + k, k % 2
                if not (last and k + 2 >= U):
                    prep(i + (k + 2) // U, (k + 2) % U)
                pool.wait_ge(y_copied, j + 1)
                after(pool, sg_ready, j - 1)
                nc.gpsimd.tensor_tensor(s2[:, b, 0:H], ysb2[:, b, 0:H], ysb2[:, b, H:E], ALU.add)
                nc.gpsimd.tensor_tensor(s2[:, b, H:E], ysb2[:, b, 0:H], ysb2[:, b, H:E], ALU.subtract).then_inc(s_ready, 1)
                pool.wait_ge(sg_ready, j + 1)
                after(pool, stored[b], 16 * (i * (U // 2) + k // 2))
                nc.gpsimd.tensor_tensor(o2[:, b], sg2[:, b], x2[:, k], ALU.add).then_inc(o_ready, 1)
            prep(0, 0)
            prep(0, 1)
            rounds(pool, T // U, step)

        @block.scalar
        def _(act):
            act.wait_ge(d_ready, 1)
            nc.scalar.activation(v["sd"], v["ve"], ACT.Sqrt).then_inc(act_setup, 1)
            act.wait_ge(d_ready, 2)
            nc.scalar.activation(v["ly"], v["cnt"], ACT.Ln).then_inc(act_setup, 1)
            act.wait_ge(d_ready, 3)
            nc.scalar.activation(v["s1"], v["arg"], ACT.Sin, scale=0.5)
            nc.scalar.activation(v["q1"], v["arg"], ACT.Sin, scale=0.25)
            nc.scalar.activation(v["q2"], v["ph"], ACT.Sin, scale=0.5).then_inc(act_setup, 1)
            for s in range(2):
                act.wait_ge(c_mm, s + 1)
                cps = psum[:, s].rearrange("p (k h) -> p k h", k=CH)
                nc.scalar.activation(cf[:, s], cps, ACT.Copy)
                nc.scalar.activation(c_hi[:, s], cps, ACT.Copy).then_inc(c_copied, 1)
            act.wait_ge(m_mm, 1)
            nc.scalar.activation(msb, psum[:, 2, 0:C * GOLAY_N].rearrange("p (c n) -> p c n", c=C), ACT.Copy,
                                 scale=1.0 / CS).then_inc(m_copied, 1)
            act.wait_ge(rt_mm, 1)
            nc.scalar.activation(wcat[:, :, 0:NE], psum[:, 3, 0:C * NE].rearrange("p (c n) -> p c n", c=C),
                                 ACT.Copy).then_inc(m_copied, 1)
            for e in range(NE):
                act.wait_ge(wscale_ready, e // LH + 1)
                act.wait_ge(wpm_ready, e + 1)
                nc.scalar.activation(w_hi[:, e], wpm[:, e % 2], ACT.Copy, scale=wscale[:, e:e + 1]).then_inc(whi_ready, 1)

            def sqrt(i, k):
                act.wait_ge(var_ready, i * U + k + 1)
                nc.scalar.activation(rt1[:, k % 2, 1], rt1[:, k % 2, 0], ACT.Sqrt).then_inc(sd_ready, 1)

            def step1(i, k, last=False):
                for q in range(GT):
                    t = (i * U + k) * GT + q
                    act.wait_ge(t1_done, t + 1)
                    after(act, mm1_done, t - 1)
                    nc.scalar.activation(xnT1[:, q % 2], psum[:, q % 2], ACT.Copy).then_inc(t1_copied, 1)
                    if q == 1 and not (last and k + 1 >= U):
                        sqrt(i + (k + 1) // U, (k + 1) % U)
            sqrt(0, 0)
            rounds(act, NG // U, step1)

            act.wait_ge(dx_ready, 1)
            nc.scalar.activation(ex, l2, ACT.Exp)
            nc.scalar.activation(e2, d2, ACT.Exp).then_inc(exp_ready, 1)

            def front(i, k):
                j, b = i * U + k, k % 2
                act.wait_ge(uvT_done, j + 1)
                after(act, y_done, j - 1)
                nc.scalar.activation(hi2[:, b], psum[:, 0].rearrange("p (c n) -> p c n", c=C), ACT.Copy)
                nc.scalar.activation(bT2[:, b], psum[0:96, 1, 0:P // 2].bitcast(BF16), ACT.Copy).then_inc(hi_ready, 1)

            def step(i, k, last=False):
                j, b = i * U + k, k % 2
                if not (last and k + 1 >= U):
                    front(i + (k + 1) // U, (k + 1) % U)
                act.wait_ge(e_used, NE * (j + 1))
                after(act, sg_ready, j - 1)
                nc.scalar.activation(g2[:, b], z2[:, b], ACT.Silu).then_inc(g_ready, 1)
                act.wait_ge(y_done, j + 1)
                after(act, s_ready, j - 1)
                nc.scalar.activation(ysb2[:, b], psum[:, 2 + b], ACT.Copy, scale=1.0 / (XS * CS)).then_inc(y_copied, 1)
            front(0, 0)
            rounds(act, T // U, step)

        @block.vector
        def _(dve):
            n = [0]

            def link(ins):
                n[0] += 1
                ins.then_inc(dch, 1)
                dve.wait_ge(dch, n[0])
            V = nc.vector
            dve.wait_ge(ld_x01, 16)
            for r in range(2):
                last = V.bn_stats(v["st"][:, r], x01[:, r * E:(r + 1) * E])
            link(last)
            for r in range(2):
                last = V.bn_aggr(v["mv"][:, r], v["st"][:, r])
            link(last)
            V.tensor_scalar(v["ve"], v["mv"][:, :, 1], EPS, None, ALU.add).then_inc(d_ready, 1)
            dve.wait_ge(act_setup, 1)
            link(V.reciprocal(v["r0"], v["sd"]))
            link(V.tensor_tensor(v["rt"], v["r0"], v["r0"], ALU.mult))
            link(V.tensor_tensor(v["rt"], v["rt"], v["ve"], ALU.mult))
            link(V.tensor_scalar(v["rt"], v["rt"], -0.5, 1.5, ALU.mult, ALU.add))
            link(V.tensor_tensor(v["r0"], v["r0"], v["rt"], ALU.mult))
            for r in range(2):
                last = V.tensor_scalar(junk[:, r * E:(r + 1) * E], x01[:, r * E:(r + 1) * E], v["mv"][:, r, 0:1],
                                       v["r0"][:, r:r + 1], ALU.subtract, ALU.mult)
            link(last)
            for c, side in enumerate(BLOCKS):
                last = V.tensor_reduce(v["mu"][:, c:c + 1], junk[:, 0:side * side], AXX, ALU.add)
            link(last)
            for c, side in enumerate(BLOCKS):
                last = V.tensor_scalar(v["mu"][:, c:c + 1], v["mu"][:, c:c + 1], 1.0 / (side * side), None, ALU.mult)
            link(last)
            for c, side in enumerate(BLOCKS):
                link(V.tensor_scalar(x01[:, 0:side * side], junk[:, 0:side * side], v["mu"][:, c:c + 1], 0.0, ALU.is_gt,
                                     ALU.add, accum_out=v["cnt"][:, c:c + 1]))
            V.tensor_scalar(v["cnt"], v["cnt"], 1.0, None, ALU.max).then_inc(d_ready, 1)
            dve.wait_ge(ld_cst, 16)
            dve.wait_ge(act_setup, 2)
            link(V.tensor_tensor(v["ly"], v["ly"], slope_c, ALU.mult))
            link(V.tensor_reduce(v["D"], v["ly"], AXX, ALU.add))
            link(V.tensor_scalar(v["D"], v["D"], 1.0, 2.0, ALU.max, ALU.min))
            V.tensor_scalar(v["wD"], v["D"], 0.2, 1.0, ALU.mult, ALU.add)
            V.tensor_scalar(v["a"], v["D"], 0.5, 1.0, ALU.mult, ALU.add)
            V.tensor_scalar(v["b"], v["D"], 0.1, None, ALU.mult)
            link(V.tensor_tensor(v["ph"], ka, ka, ALU.mult))
            link(V.tensor_tensor(v["wD"], v["wD"], v["D"], ALU.mult))
            V.tensor_scalar(v["arg"], ka, v["a"], v["wD"], ALU.mult, ALU.add)
            link(V.scalar_tensor_tensor(v["ph"], v["ph"], v["b"], ka, ALU.mult, ALU.subtract))
            V.tensor_scalar(v["ph"], v["ph"], v["wD"], None, ALU.add).then_inc(d_ready, 1)
            dve.wait_ge(act_setup, 3)
            V.tensor_tensor(v["q1"], v["q1"], v["q1"], ALU.mult)
            link(V.tensor_tensor(v["q2"], v["q2"], v["q2"], ALU.mult))
            V.tensor_scalar(v["q1"], v["q1"], -2.0, 1.0, ALU.mult, ALU.add)
            link(V.tensor_scalar(v["q2"], v["q2"], -2.0, 1.0, ALU.mult, ALU.add))
            link(V.tensor_tensor(v["q1"], v["q1"], v["q2"], ALU.mult))
            link(V.tensor_tensor(v["q1"], v["q1"], v["s1"], ALU.mult))
            link(V.tensor_tensor(v["q1"], v["q1"], kw, ALU.mult))
            for c in range(C):
                last = V.tensor_scalar(tabf[:, c], tab[:, c], v["q1"][:, c:c + 1], 2.0 * CS, ALU.mult, ALU.mult)
            last.then_inc(filt_ready, 1)
            dve.wait_ge(ld_small, 16 * 8)
            V.tensor_tensor(welpm[:, 0:CH], welraw[:, 0:CH], welraw[:, CH:C], ALU.add)
            V.tensor_tensor(welpm[:, CH:C], welraw[:, 0:CH], welraw[:, CH:C], ALU.subtract).then_inc(wel_ready, 1)
            V.tensor_scalar(bel[:, :], bel[:, :], -1.0, None, ALU.mult)
            V.tensor_tensor(wlpm[:, 0:H], wle[:, 0:H], wle[:, H:E], ALU.add)
            link(V.tensor_tensor(wlpm[:, H:E], wle[:, 0:H], wle[:, H:E], ALU.subtract))
            half = XS * CS / 2
            link(V.tensor_scalar(wlh, wlpm, half, None, ALU.mult))
            link(V.scalar_tensor_tensor(wlr, wlpm, half, wlh, ALU.mult, ALU.subtract))
            link(V.tensor_copy(wlm, wlr))
            V.tensor_copy(wle3[0:32], wlh[0:32])
            V.tensor_copy(wle3[32:64], wlm[32:64])
            V.tensor_tensor(wle3[64:96], wlr[64:96], wlm[64:96], ALU.subtract).then_inc(wle_ready, 1)
            for s in range(2):
                dve.wait_ge(c_copied, s + 1)
                V.tensor_tensor(c_lo[:, s], psum[:, s].rearrange("p (k h) -> p k h", k=CH), c_hi[:, s],
                                ALU.subtract).then_inc(c_lo_ready, 1)
            dve.wait_ge(m_copied, 2)
            V.tensor_tensor(wcat[:, 0:CH, NE:NL], msb[:, 0:CH], msb[:, CH:C], ALU.add)
            V.tensor_tensor(wcat[:, CH:C, NE:NL], msb[:, 0:CH], msb[:, CH:C], ALU.subtract).then_inc(wcat_raw, 1)
            dve.wait_ge(wmean_mm, 1)
            V.tensor_tensor(wcat[:, :, :], wcat[:, :, :], psum[:, 4, 0:NL].unsqueeze(1).broadcast_to([P, C, NL]),
                            ALU.subtract).then_inc(wcat_ready, 1)

            for half_no in range(NE // LH):
                for e in range(LH * half_no, LH * half_no + LH):
                    dve.wait_ge(ld_w[e % LH], 16 * (half_no + 1))
                    V.tensor_reduce(amax[:, e:e + 1], raw[:, e % LH].rearrange("p c e -> p (c e)"), AXX, ALU.max,
                                    apply_absolute_value=True).then_inc(amax_ready, 1)
                dve.wait_ge(amax_red, half_no + 1)
                hs = slice(LH * half_no, LH * half_no + LH)
                link(V.tensor_scalar(amax_all[:, hs], amax_all[:, hs], 1e-25, None, ALU.max))
                link(V.reciprocal(wscale[:, hs], amax_all[:, hs]))
                V.tensor_scalar(unscale[:, hs], amax_all[:, hs], 0.5 / (XS * WS), None, ALU.mult)
                ins = V.tensor_scalar(wscale[:, hs], wscale[:, hs], WS, None, ALU.mult)
                ins.then_inc(wscale_ready, 1)
                dve.wait_ge(wscale_ready, half_no + 1)
                for e in range(LH * half_no, LH * half_no + LH):
                    dve.wait_ge(whi_ready, e + 1)
                    V.scalar_tensor_tensor(w_lo[:, e], wpm[:, e % 2], wscale[:, e:e + 1], w_hi[:, e], ALU.mult,
                                           ALU.subtract).then_inc(wlo_ready, 1)

            def stats(i, k):
                dve.wait_ge(ld_x[k], 16 * (i + 1))
                for q in range(GT):
                    last = V.bn_stats(st6[:, k % 2, q], xbuf[:, k, q])
                last.then_inc(stats_ready, 1)

            def aggregate(i, k):
                g, b = i * U + k, k % 2
                for q in range(GT):
                    last = V.bn_aggr(mv1[:, b, q], st6[:, b, q])
                last.then_inc(aggr_ready, 1)
                dve.wait_ge(aggr_ready, g + 1)
                V.tensor_scalar(rt1[:, b, 0], mv1[:, b, :, 1], EPS, None, ALU.add).then_inc(var_ready, 1)
                V.tensor_scalar(mean[:, bass.ds(g * GT, GT)], mv1[:, b, :, 0], 2.0, None, ALU.mult)

            def lat_scale(i, k):
                g = i * U + k
                dve.wait_ge(mm1_done, (g + 1) * GT)
                V.tensor_tensor(lat[:, :, bass.ds(g * GT, GT)],
                                psum[:, 2 + k % 2, 0:GT * NL].rearrange("p (t n) -> p n t", t=GT),
                                rstd[:, bass.ds(g * GT, GT)].unsqueeze(1).broadcast_to([P, NL, GT]),
                                ALU.mult).then_inc(lat_copied, 1)

            def step1(i, k, last=False):
                g, b = i * U + k, k % 2
                ahead = not (last and k + 1 >= U)
                nxt = (i + (k + 1) // U, (k + 1) % U)
                if ahead:
                    stats(*nxt)
                    dve.wait_ge(stats_ready, g + 2)
                dve.wait_ge(sd_ready, g + 1)
                ve, sd, r0, rt = (rt1[:, b, c] for c in range(4))
                V.reciprocal(r0, sd).then_inc(newton, 1)
                if ahead:
                    aggregate(*nxt)
                dve.wait_ge(newton, 4 * g + 1)
                V.tensor_tensor(rt, r0, r0, ALU.mult).then_inc(newton, 1)
                dve.wait_ge(newton, 4 * g + 2)
                V.tensor_tensor(rt, rt, ve, ALU.mult).then_inc(newton, 1)
                dve.wait_ge(newton, 4 * g + 3)
                V.tensor_scalar(rt, rt, -0.5, 1.5, ALU.mult, ALU.add).then_inc(newton, 1)
                dve.wait_ge(newton, 4 * g + 4)
                V.tensor_tensor(rstd[:, bass.ds(g * GT, GT)], r0, rt, ALU.mult).then_inc(rstd_ready, 1)
                if not (isinstance(i, int) and i == 0 and k == 0):
                    dve.wait_ge(rstd_ready, g)
                    lat_scale(i - (k == 0), (k - 1) % U)
            stats(0, 0)
            dve.wait_ge(stats_ready, 1)
            aggregate(0, 0)
            rounds(dve, NG // U, step1)
            dve.wait_ge(rstd_ready, NG)
            lat_scale(NG // U - 1, U - 1)

            dve.wait_ge(lat_copied, NG)
            dve.wait_ge(t1_done, T)
            lg = lat[:, 0:NE]

            def over_e(a):
                return a.rearrange("p n t -> p t n")

            def each(a, m=NE):
                return a.unsqueeze(1).broadcast_to([P, m, T])
            ramp_b = ramp.unsqueeze(2).broadcast_to([P, NE, T])

            def one_hot(m, logits, mx, oh):
                link(V.tensor_reduce(m, over_e(logits), AXX, ALU.max))
                link(V.tensor_tensor(eq, logits, each(m), ALU.is_equal))
                link(V.tensor_tensor(sc, eq, ramp_b, ALU.mult))
                link(V.tensor_reduce(mx, over_e(sc), AXX, ALU.max))
                link(V.tensor_tensor(oh, sc, each(mx), ALU.is_equal))
            one_hot(m1, lg, mx1, oh1)
            link(V.scalar_tensor_tensor(l2, oh1, -3e38, lg, ALU.mult, ALU.add))
            one_hot(m2, l2, mx2, oh2)
            V.tensor_tensor(d2, m2, m1, ALU.subtract)
            V.tensor_tensor(l2, lg, each(m1), ALU.subtract).then_inc(dx_ready, 1)
            link(V.tensor_tensor(bits, lat[:, NE:NL], bel[:, :].unsqueeze(2).broadcast_to([P, GOLAY_N, T]), ALU.is_gt))
            V.tensor_reduce(nlow, over_e(bits[:, 0:GOLAY_R]), AXX, ALU.add)
            link(V.tensor_reduce(nhigh, over_e(bits[:, GOLAY_R:]), AXX, ALU.add))
            link(V.scalar_tensor_tensor(fix, nlow, 4.0, nhigh, ALU.mult, ALU.add))
            link(V.tensor_scalar(fix, fix, 3.0, None, ALU.is_le))
            link(V.tensor_tensor(fixadd, bits[:, GOLAY_R:], each(fix, GOLAY_R), ALU.mult))
            V.tensor_tensor(bits[:, 0:GOLAY_R], bits[:, 0:GOLAY_R], fixadd, ALU.add).then_inc(corr_ready, 1)
            dve.wait_ge(exp_ready, 1)
            link(V.tensor_reduce(zs, over_e(ex), AXX, ALU.add))
            link(V.reciprocal(p1, zs))
            link(V.tensor_tensor(p2, e2, p1, ALU.mult))
            link(V.tensor_tensor(den, p1, p2, ALU.add))
            link(V.tensor_scalar(den, den, 1e-6, None, ALU.add))
            link(V.reciprocal(den, den))
            V.tensor_tensor(w1, p1, den, ALU.mult)
            link(V.tensor_tensor(w2, p2, den, ALU.mult))
            V.tensor_tensor(p1, p1, w1, ALU.mult)
            link(V.tensor_tensor(p2, p2, w2, ALU.mult))
            V.tensor_tensor(info[:, :, 2], p1, p2, ALU.add)
            V.tensor_copy(info[:, :, 0], mean[:, :])
            V.tensor_scalar(info[:, :, 1], rstd[:, :], XS, None, ALU.mult)
            V.tensor_tensor(oh1, oh1, each(w1), ALU.mult)
            link(V.tensor_tensor(oh2, oh2, each(w2), ALU.mult))
            link(V.tensor_tensor(oh1, oh1, oh2, ALU.add))
            dve.wait_ge(corr_ready, 2)
            V.tensor_tensor(over_e(info[:, :, 8:16]), oh1, unscale[:, :].unsqueeze(2).broadcast_to([P, NE, T]),
                            ALU.mult).then_inc(info_ready, 1)

            def norm(i, k):
                j, b = i * U + k, k % 2
                dve.wait_ge(raw_ready, j + 1)
                after(dve, uvT_done, j - 1)
                V.tensor_scalar(uv2[:, b, 0:H], raw2[:, b, 0:H], inf2[:, k, 0:1], inf2[:, k, 1:2], ALU.subtract, ALU.mult)
                V.tensor_scalar(uv2[:, b, H:E], raw2[:, b, H:E], inf2[:, k, 1:2], None, ALU.mult).then_inc(uv_ready, 1)

            def front(i, k):
                j, b = i * U + k, k % 2
                dve.wait_ge(hi_ready, j + 1)
                after(dve, y_done, j - 1)
                V.tensor_tensor(lo2[:, b], psum[:, 0].rearrange("p (c n) -> p c n", c=C), hi2[:, b],
                                ALU.subtract).then_inc(lo_ready, 1)

            def step(i, k, last=False):
                j, b = i * U + k, k % 2
                if not (last and k + 2 >= U):
                    norm(i + (k + 2) // U, (k + 2) % U)
                if not (last and k + 1 >= U):
                    front(i + (k + 1) // U, (k + 1) % U)
                after(dve, g_ready, j - 1)
                for e in range(NE):
                    dve.wait_ge(e_done, NE * j + e + 1)
                    wj = inf2[:, k, 8 + e:9 + e]
                    ps = psum[:, 4 + e % 4]
                    if e == 0:
                        ins = V.tensor_scalar(z2[:, b], ps, wj, inf2[:, k, 2:3], ALU.mult, ALU.add)
                    else:
                        dve.wait_ge(e_used, NE * j + e)
                        ins = V.scalar_tensor_tensor(z2[:, b], ps, wj, z2[:, b], ALU.mult, ALU.add)
                    ins.then_inc(e_used, 1)
                dve.wait_ge(s_ready, j + 1)
                dve.wait_ge(g_ready, j + 1)
                after(dve, o_ready, j - 1)
                V.tensor_tensor(sg2[:, b], s2[:, b], g2[:, b], ALU.mult).then_inc(sg_ready, 1)
            norm(0, 0)
            norm(0, 1)
            front(0, 0)
            rounds(dve, T // U, step)

        @block.tensor
        def _(pe):
            pe.wait_ge(ident_ready, 2)
            pe.wait_ge(ld_router, 16)
            for c in range(C):
                last = nc.tensor.transpose(psum[:, 3, c * NE:(c + 1) * NE], rtr[:, c * P:(c + 1) * P], ident[0:NE, 0:NE])
            last.then_inc(rt_mm, 1)
            pe.wait_ge(filt_ready, 1)
            for s in range(2):
                for ih in range(CH):
                    for kc in range(CH):
                        last = nc.tensor.matmul(psum[:, s, ih * H:(ih + 1) * H], tabf[:, 2 * s + kc, ih * P:(ih + 1) * P],
                                                tab[:, 2 * s + kc], start=(kc == 0), stop=(kc == CH - 1))
                last.then_inc(c_mm, 1)
            pe.wait_ge(wel_ready, 1)
            for s in range(2):
                pe.wait_ge(c_copied, s + 1)
                for ih in range(CH):
                    m = 2 * s + ih
                    for kc in range(CH):
                        last = nc.tensor.matmul(psum[:, 2, m * GOLAY_N:(m + 1) * GOLAY_N], cf[:, s, kc, ih * P:(ih + 1) * P],
                                                welpm[:, 2 * s + kc], start=(kc == 0), stop=(kc == CH - 1))
            last.then_inc(m_mm, 1)

            pe.wait_ge(wcat_raw, 1)
            pe.wait_ge(ones_ready, 1)
            for c in range(C):
                last = nc.tensor.matmul(psum[:, 4, 0:NL], avg[:, :], wcat[:, c], start=(c == 0), stop=(c == C - 1))
            last.then_inc(wmean_mm, 1)

            pe.wait_ge(c_lo_ready, 2)
            pe.wait_ge(wcat_ready, 1)

            def turn(i, k, q):
                t = (i * U + k) * GT + q
                if q == 0:
                    pe.wait_ge(ld_x[k], 16 * (i + 1))
                after(pe, t1_copied, t - 1)
                for c in range(C):
                    last = nc.tensor.transpose(psum[:, q % 2, c * P:(c + 1) * P], xbuf[:, k, q, c * P:(c + 1) * P], ident[:, :])
                last.then_inc(t1_done, 1)

            def step1(i, k, last=False):
                g = i * U + k
                for q in range(GT):
                    nq = k * GT + q + 1
                    if not (last and nq >= U * GT):
                        turn(i + nq // (U * GT), nq // GT % U, nq % GT)
                    pe.wait_ge(t1_copied, g * GT + q + 1)
                    if q == 0:
                        after(pe, lat_copied, g - 1)
                    for c in range(C):
                        mm = nc.tensor.matmul(psum[:, 2 + k % 2, q * NL:(q + 1) * NL], xnT1[:, q % 2, c * P:(c + 1) * P],
                                              wcat[:, c], start=(c == 0), stop=(c == C - 1))
                    mm.then_inc(mm1_done, 1)
            turn(0, 0, 0)
            rounds(pe, NG // U, step1)

            pe.wait_ge(t1_copied, T)
            pe.wait_ge(lat_copied, NG)
            pe.wait_ge(wlo_ready, NE)

            def front(i, k):
                j, b = i * U + k, k % 2
                pe.wait_ge(uv_ready, j + 1)
                after(pe, lo_ready, j)
                nc.tensor.transpose(psum[0:96, 1, 0:P // 2].bitcast(BF16), inf2[:, k, 16:64].bitcast(BF16), ident_b[:, :])
                for c in range(C):
                    last = nc.tensor.transpose(psum[:, 0, c * P:(c + 1) * P], uv2[:, b, c * P:(c + 1) * P], ident[:, :])
                last.then_inc(uvT_done, 1)

            def step(i, k, last=False):
                j, b = i * U + k, k % 2
                if not (last and k + 1 >= U):
                    front(i + (k + 1) // U, (k + 1) % U)
                pe.wait_ge(lo_ready, j + 1)
                for e in range(NE):
                    after(pe, e_used, NE * j + e - 3)
                    ps = psum[:, 4 + e % 4]
                    for c in range(C):
                        nc.tensor.matmul(ps, hi2[:, b, c], w_hi[:, e, c], start=(c == 0), stop=False)
                        nc.tensor.matmul(ps, hi2[:, b, c], w_lo[:, e, c], start=False, stop=False)
                        mm = nc.tensor.matmul(ps, lo2[:, b, c], w_hi[:, e, c], start=False, stop=(c == C - 1))
                    mm.then_inc(e_done, 1)
                after(pe, y_copied, j - 1)
                yb = psum[:, 2 + b]
                nc.tensor.matmul(yb, bT2[:, b], wle3[:, :], start=True, stop=False)
                for s in range(2):
                    ys = yb[:, s * H:(s + 1) * H]
                    for kc in range(CH):
                        c = s * CH + kc
                        end = s == 1 and kc == CH - 1
                        nc.tensor.matmul(ys, hi2[:, b, c], c_hi[:, s, kc], start=False, stop=False)
                        nc.tensor.matmul(ys, hi2[:, b, c], c_lo[:, s, kc], start=False, stop=False)
                        mm = nc.tensor.matmul(ys, lo2[:, b, c], c_hi[:, s, kc], start=False, stop=end)
                mm.then_inc(y_done, 1)
            front(0, 0)
            rounds(pe, T // U, step)


_INS = ["L0_attn_x", "L0_attn_W_el", "L0_attn_b_el", "L0_attn_W_le", "L0_attn_b_le", "L0_ffn_router_w",
        "L0_ffn_expert_weights"]


def kernel(**inputs):
    import concourse.bacc as bacc
    from concourse.bass_utils import run_bass_kernel_spmd as run

    nc = bacc.Bacc("TRN2", target_bir_lowering=False, num_devices=1)
    arrays, args = {}, []
    for name in _INS:
        a = np.ascontiguousarray(inputs[name])
        arrays[f"in_{name}"] = a
        args.append(nc.dram_tensor(f"in_{name}", a.shape, mybir.dt.from_np(a.dtype), kind="ExternalInput").ap())
    shape = arrays["in_L0_attn_x"].shape
    table = fourier_constants(shape[-1])
    arrays["in_consts"] = table
    args.append(nc.dram_tensor("in_consts", table.shape, F32, kind="ExternalInput").ap())
    args.append(nc.dram_tensor("out_0", shape, F32, kind="ExternalOutput").ap())
    build(nc, *args)
    r = run(nc, [arrays], core_ids=[0])
    return r.results[0]["out_0"]
```

```python
import math
from contextlib import ExitStack

import numpy as np
import concourse.bass as bass
from concourse import mybir

F32 = mybir.dt.float32
F16 = mybir.dt.float16
I32 = mybir.dt.int32
BF16 = mybir.dt.bfloat16
ALU = mybir.AluOpType
ACT = mybir.ActivationFunctionType
AXX = mybir.AxisListType.X
RMAX = bass.bass_isa.ReduceOp.max

P = 128
HALVES = 2
GOLAY_N, GOLAY_R = 24, 12
XS = 1024.0
CS = 16384.0
WS = 8192.0
EPS = 1e-5
INFO_W = 64
GT = 4
U = 4
FAR = 1 << 20
BLOCKS = (2, 4, 8, 16, 32)


def fourier_constants(E):
    H = E // 2
    n = np.arange(H)
    rows, freq, weight = [], [], []
    for odd in (0, 1):
        ks = np.arange(odd, H + 1, 2)
        for kind in (np.cos, np.sin):
            for k in ks:
                if kind is np.sin and k in (0, H):
                    continue
                rows.append(kind(2 * np.pi * ((k * n) % E) / E))
                freq.append(k / E)
                weight.append((1.0 if k in (0, H) else 2.0) / E)
    C = E // P
    table = np.asarray(rows).reshape(C, P, H).transpose(1, 0, 2).reshape(P, C * H)
    ka = np.float32(np.asarray(freq, np.float32) + np.float32(1e-8)).reshape(C, P).T
    w = np.asarray(weight).reshape(C, P).T
    lx = np.log(np.asarray(BLOCKS, np.float64))
    n = len(BLOCKS)
    slope = -(n * lx - lx.sum()) / (n * (lx * lx).sum() - lx.sum() ** 2)
    return np.concatenate([table, ka, w, np.broadcast_to(slope, (P, n))], axis=1)


def routing_constants(NE, cap, TB):
    pairs = [(a, b) for a in range(NE) for b in range(a + 1, NE)]
    first, second = np.asarray(pairs).T
    q = np.arange(len(pairs))
    ramp = NE - np.arange(NE)
    key = NE * (NE - first) + (NE - second)
    region = q * cap
    carry = np.tile(np.arange(TB) > 0, len(pairs))
    tile = np.arange(P)[:, None] + P * np.arange(2)[None, :]
    not_before = -(np.arange(P)[:, None] >= np.arange(P)[None, :]).astype(np.float64)
    same = np.concatenate([ramp, key, first, second, region, region // P, carry])
    return np.concatenate([np.broadcast_to(same, (P, same.size)), tile, not_before], axis=1)


def build(nc, x_in, W_el, b_el, W_le, b_le, router_w, experts, consts, out):
    B, S, E = x_in.shape
    NE = experts.shape[0]
    N = B * S
    T = N // P
    C = E // P
    H = E // 2
    CH = H // P
    NG = T // GT
    TB = U * GT
    R = T // TB
    NL = NE + GOLAY_N
    LH = 4
    NQ = NE * (NE - 1) // 2
    NT = -(-(T + NQ - 1) // U) * U
    TROWS = NQ * T + 2 * P

    x_rows = x_in.rearrange("b s e -> (b s) e")
    out_rows = out.rearrange("b s e -> (b s) e")
    x_tiles = x_rows.rearrange("(t p) e -> p t e", p=P)
    info_dram = nc.dram_tensor("token_info", (N, INFO_W), F32, kind="Internal").ap()
    info_tiles = info_dram.rearrange("(t p) w -> p t w", p=P)
    pair_tokens = nc.dram_tensor("pair_tokens", (TROWS, P), I32, kind="Internal").ap()
    pair_slots = pair_tokens.rearrange("r (c o) -> (r c) o", o=1)

    ctx = ExitStack()
    with ctx:
        def sb(name, shape, dt=F32):
            return ctx.enter_context(nc.sbuf_tensor(name, shape, dt))

        def sem(name):
            return ctx.enter_context(nc.semaphore(name))

        w_hi = sb("w_hi", [P, NE, C, E], F16)
        w_lo = sb("w_lo", [P, NE, C, E], F16)
        arena = sb("arena", [P, 12288])
        xbuf = sb("xbuf", [P, U, GT, E])
        xT4 = sb("xT4", [P, 2, C, GT * P])
        CW = NE + 5 * NQ + NQ * TB + 2 + P
        cst = sb("cst", [P, C * H + 2 * C + len(BLOCKS) + CW])
        c_hi = sb("c_hi", [P, 2, CH, H], F16)
        c_lo = sb("c_lo", [P, 2, CH, H], F16)
        wle3 = sb("wle3", [96, E], BF16)
        ident = sb("ident", [P, P])
        ident_b = sb("ident_b", [P, P], BF16)
        ident_h = sb("ident_h", [P, P], F16)
        wcat = sb("wcat", [P, C, P])
        avg = sb("avg", [P, P])
        amax = sb("amax", [P, NE])
        amax_all = sb("amax_all", [P, NE])
        wscale = sb("wscale", [P, NE])
        unscale = sb("unscale", [P, NE])
        bel = sb("bel", [P, GOLAY_N])
        info = sb("info", [P, TB, INFO_W])
        lat = sb("lat", [P, NL, TB])
        latT = sb("latT", [P, 2, GT * P])
        st6 = sb("st6", [P, TB, 6])
        mv1 = sb("mv1", [P, TB, 2])
        rt1 = sb("rt1", [P, 4, TB])
        rstd = sb("rstd", [P, TB])
        mean2 = sb("mean2", [P, TB])
        rsc = sb("rsc", [P, 8, NE, TB])
        rsm = sb("rsm", [P, 24, TB])
        bits = sb("bits", [P, GOLAY_N, TB])
        fixadd = sb("fixadd", [P, GOLAY_R, TB])
        pairs = sb("pairs", [P, NQ, TB], F16)
        ranks = sb("ranks", [P, NQ, TB])
        slots = sb("slots", [P, NQ, TB])
        used = sb("used", [P, NQ])
        tokf = sb("tokf", [P, TB])
        tok = sb("tok", [P, 2, TB], I32)
        slot = sb("slot", [P, 2, TB], I32)
        nbefore = sb("nbefore", [P, P], F16)
        ones = sb("ones", [P, P], F16)
        tq = sb("tq", [P, 3, NQ])
        tcmp = sb("tcmp", [P, 2, NQ + 1])
        tone = sb("tone", [P, 2, NQ])
        tmul = sb("tmul", [P, 2, NQ])
        tval = sb("tval", [P, 3, 2])
        trow = sb("trow", [P, 2], I32)
        tokT = sb("tokT", [P, 2, P], I32)
        tokTf = sb("tokTf", [P, 2, P])
        tile_tok = sb("tile_tok", [P, 2 * P], I32)
        tile_exp = sb("tile_exp", [1, 2, 2 * P], I32)
        gidx = sb("gidx", [P, U], I32)
        sidx = sb("sidx", [P, U], I32)
        small = sb("small", [P, 256])
        psum = ctx.enter_context(nc.psum_tensor("banks", [P, 8, 512], F32))

        tab = cst[:, 0:C * H].rearrange("p (c h) -> p c h", c=C)
        o = C * H
        ka, kw = cst[:, o:o + C], cst[:, o + C:o + 2 * C]
        o += 2 * C
        slope_c = cst[:, o:o + len(BLOCKS)]
        o += len(BLOCKS)
        ramp = cst[:, o:o + NE]
        o += NE
        key_c, first_c, second_c, region_c, row_c = (cst[:, o + NQ * i:o + NQ * (i + 1)] for i in range(5))
        o += 5 * NQ
        carry_c = cst[:, o:o + NQ * TB]
        o += NQ * TB
        tile_c = cst[:, o:o + 2]
        nbefore_c = cst[:, o + 2:o + 2 + P]

        raw = arena[:, 0:8192].rearrange("p (s c e) -> p s c e", s=LH, c=C)
        wpm = arena[:, 8192:12288].rearrange("p (s c e) -> p s c e", s=2, c=C)
        xb = xbuf[:, :, :, :].rearrange("p u t e -> p (u t e)")
        x01 = xb[:, 0:1024]
        junk = xb[:, 1024:2048]
        tabf = xb[:, 2048:3072].rearrange("p (c h) -> p c h", c=C)
        cf = xb[:, 3072:4096].rearrange("p (s k h) -> p s k h", s=2, k=CH)
        welraw = xb[:, 4096:4096 + C * GOLAY_N].rearrange("p (c n) -> p c n", c=C)
        welpm = xb[:, 4224:4224 + C * GOLAY_N].rearrange("p (c n) -> p c n", c=C)
        msb = xb[:, 4352:4352 + C * GOLAY_N].rearrange("p (c n) -> p c n", c=C)
        rtr = xb[0:NE, 4608:4608 + E]
        wle = xb[0:96, 5120:5120 + E]
        wlpm = xb[0:96, 5632:5632 + E]
        wlh = xb[0:96, 6144:6144 + E // 2].bitcast(BF16)
        wlr = xb[0:96, 6656:6656 + E]
        wlm = xb[0:96, 7168:7168 + E // 2].bitcast(BF16)
        lg = lat[:, 0:NE]
        eq, sc, oh1, oh2, l2, ex, dl, ux = (rsc[:, i] for i in range(8))
        (m1, m2, mx1, mx2, zs, d2, e2, p1, p2, den, w1, w2, u1, u2, nlow, nhigh, fix, kmax, kmin, isa, isb,
         wt1, wt2, slotf) = (rsm[:, i] for i in range(24))
        far = xT4[:, :, :, :].rearrange("p b c n -> p (b c n)").bitcast(I32)[:, 0:TROWS]
        info_bits = info[:, :, 16:64].bitcast(BF16).rearrange("p t (g c) -> p t g c", g=3)

        def two(t, i):
            return t[:, i:i + 2 * E].rearrange("p (s e) -> p s e", s=2)

        def two16(t, i):
            return t[:, i:i + E].bitcast(F16).rearrange("p (s e) -> p s e", s=2)
        x2 = xb[:, 0:U * E].rearrange("p (s e) -> p s e", s=U)
        raw2, uv2, o2, ysb2, s2, sg2 = (two(xb, U * E + 2 * E * i) for i in range(6))
        t2, z2, g2 = (two(arena, 2 * E * i) for i in range(3))
        hi2, lo2 = (two16(arena, 6 * E + E * i) for i in range(2))
        hl2 = arena[:, 8 * E:10 * E].bitcast(F16).rearrange("p (s v c e) -> p s v c e", s=2, v=2, c=C)
        bT2 = arena[0:96, 10 * E:10 * E + P].bitcast(BF16).rearrange("p (s e) -> p s e", s=2)
        inf2 = arena[:, 11 * E:11 * E + U * INFO_W].rearrange("p (s w) -> p s w", s=U)

        v, at = {}, 0
        for name, m in (("st", 12), ("mv", 4), ("ve", 2), ("sd", 2), ("r0", 2), ("rt", 2), ("mu", 5), ("cnt", 5), ("ly", 5),
                        ("D", 1), ("wD", 1), ("a", 1), ("b", 1), ("arg", C), ("ph", C), ("s1", C), ("q1", C), ("q2", C)):
            v[name] = small[:, at:at + m]
            at += m
        v["st"] = v["st"].rearrange("p (r k) -> p r k", r=2)
        v["mv"] = v["mv"].rearrange("p (r k) -> p r k", r=2)

        def sems(names):
            return [sem(x) for x in names.split()]
        ld_x01, ld_cst, ld_small, ld_router = sems("ld_x01 ld_cst ld_small ld_router")
        ld_w = [sem(f"ld_w{i}") for i in range(LH)]
        ld_x = [sem(f"ld_x{i}") for i in range(U)]
        dch, pch, d_ready, act_setup, filt_ready = sems("vector_chain pool_chain d_ready act_setup filt_ready")
        ident_ready, ones_ready, info_init, zeroed, far_ready, far_stored = sems(
            "ident_ready ones_ready info_init zeroed far_ready far_stored")
        c_mm, c_copied, c_lo_ready, m_mm, wel_ready, m_copied, rt_mm, wcat_raw, wmean_mm, wcat_ready, wle_ready = sems(
            "c_mm c_copied c_lo_ready m_mm wel_ready m_copied rt_mm wcat_raw wmean_mm wcat_ready wle_ready")
        amax_ready, amax_red, wscale_ready, wpm_ready, whi_ready, wlo_ready = sems(
            "amax_ready amax_red wscale_ready wpm_ready whi_ready wlo_ready")
        sort_init, iota_ready = sems("sort_init iota_ready")
        t1_done, t1_copied, mm1_done, latT_copied, back_done, lat_copied = sems(
            "t1_done t1_copied mm1_done latT_copied back_done lat_copied")
        stats_ready, aggr_ready, var_ready, sd_ready, newton, rstd_ready = sems(
            "stats_ready aggr_ready var_ready sd_ready newton rstd_ready")
        route_a, route_c, route_d, dx_ready, exp_ready, corr_ready, bits_copied = sems(
            "route_a route_c route_d dx_ready exp_ready corr_ready bits_copied")
        pairs_ready, rank_mm, slot_ready, scattered, info_ready, info_stored = sems(
            "pairs_ready rank_mm slot_ready scattered info_ready info_stored")
        slot_seen, latT_seen, o_seen = sems("slot_seen latT_seen o_seen")
        rows_ready, rows_loaded, rows_float, rows_turned, exps_mm, tiles_ready = sems(
            "rows_ready rows_loaded rows_float rows_turned exps_mm tiles_ready")
        ld_x2 = [sem(f"ld_x2_{i}") for i in range(U)]
        stored = [sem(f"stored{i}") for i in range(2)]
        inf_init, gidx_ready, sidx_ready, raw_ready, uv_ready, hi_ready, split_ready = sems(
            "inf_init gidx_ready sidx_ready raw_ready uv_ready hi_ready split_ready")
        uvT_done, hl_ready, e_done, t_ready, z_ready, g_ready, y_done, y_copied, s_ready, sg_ready, o_ready = sems(
            "uvT_done hl_ready e_done t_ready z_ready g_ready y_done y_copied s_ready sg_ready o_ready")

        block = ctx.enter_context(nc.Block())

        def after(eng, s, v):
            if isinstance(v, int) and v <= 0:
                return
            eng.wait_ge(s, v)

        def rounds(eng, count, step, head=1):
            for i in range(head):
                for k in range(U):
                    step(i, k)
            with eng.Fori(head, count - 1) as i:
                for k in range(U):
                    step(i, k)
            for k in range(U):
                step(count - 1, k, last=True)

        def at(i, k, ahead):
            return i + (k + ahead) // U, (k + ahead) % U

        def later_than_first(i):
            return not (isinstance(i, int) and i == 0)

        @block.sync
        def _(sp):
            sp.dma_start(x01, x_rows[0:2, :].rearrange("n e -> (n e)").partition_broadcast(P)).then_inc(ld_x01, 16)
            sp.dma_start(cst[:, :], consts).then_inc(ld_cst, 16)
            sp.dma_start(welraw, W_el.rearrange("(c p) n -> p c n", p=P)).then_inc(ld_small, 16)
            sp.dma_start(bel[:, :], b_el.partition_broadcast(P)).then_inc(ld_small, 16)
            sp.wait_ge(zeroed, 1)
            for g in range(3):
                sp.dma_start(wle[32 * g:32 * g + GOLAY_N, :], W_le).then_inc(ld_small, 16)
                sp.dma_start(wle[32 * g + GOLAY_N:32 * g + GOLAY_N + 1, :], b_le.rearrange("(a e) -> a e", a=1)).then_inc(ld_small, 16)
            sp.dma_start(rtr, router_w).then_inc(ld_router, 16)
            for e in range(NE):
                if e >= LH:
                    sp.wait_ge(wpm_ready, e - LH + 1)
                sp.dma_start(raw[:, e % LH], experts[e].rearrange("(c p) o -> p c o", p=P)).then_inc(ld_w[e % LH], 16)
            sp.wait_ge(far_ready, 1)
            sp.dma_start(pair_tokens.rearrange("(p r) c -> p (r c)", p=P), far).then_inc(far_stored, 16)
            sp.wait_ge(wcat_ready, 1)
            sp.wait_ge(wle_ready, 1)

            def load(i, k):
                after(sp, t1_done, GT * ((i - 1) * U + k + 1))
                after(sp, stats_ready, (i - 1) * U + k + 1)
                sp.dma_start(xbuf[:, k], x_tiles[:, bass.ds((i * U + k) * GT, GT), :]).then_inc(ld_x[k], 16)
            for k in range(U):
                load(0, k)
            with sp.Fori(1, R) as i:
                for k in range(U):
                    load(i, k)

        @block.gpsimd
        def _(pool):
            G = nc.gpsimd
            n = [0]

            def link(ins):
                n[0] += 1
                ins.then_inc(pch, 1)
                pool.wait_ge(pch, n[0])
            G.memset(wle, 0.0).then_inc(zeroed, 1)
            G.memset(wcat[:, :, :], 0.0).then_inc(zeroed, 1)
            G.memset(avg[:, :], 1.0 / E)
            G.memset(ones[:, :], 1.0).then_inc(ones_ready, 1)
            link(G.memset(ident[:, :], 0.0))
            G.affine_select(out=ident[:, :], in_=ident[:, :], compare_op=ALU.not_equal, fill=1.0, base=0,
                            pattern=[[-1, P]], channel_multiplier=1).then_inc(ident_ready, 1)
            pool.wait_ge(ident_ready, 1)
            G.tensor_copy(ident_b[:, :], ident[:, :])
            G.tensor_copy(ident_h[:, :], ident[:, :]).then_inc(ident_ready, 1)
            G.memset(far, FAR).then_inc(far_ready, 1)
            G.iota(tok[:, 0, :], pattern=[[P, TB]], base=-P * TB, channel_multiplier=1).then_inc(iota_ready, 1)
            link(G.memset(info[:, :, :], 0.0))
            G.memset(info_bits[:, :, :, GOLAY_N:GOLAY_N + 1], 1.0).then_inc(info_init, 1)
            for half in range(NE // LH):
                pool.wait_ge(amax_ready, LH * (half + 1))
                hs = slice(LH * half, LH * half + LH)
                G.partition_all_reduce(amax_all[:, hs], amax[:, hs], P, RMAX).then_inc(amax_red, 1)
                for e in range(LH * half, LH * half + LH):
                    after(pool, whi_ready, e - 1)
                    after(pool, wlo_ready, e - 1)
                    r, w = raw[:, e % LH], wpm[:, e % 2]
                    G.tensor_tensor(w[:, 0:CH], r[:, 0:CH], r[:, CH:C], ALU.add)
                    G.tensor_tensor(w[:, CH:C], r[:, 0:CH], r[:, CH:C], ALU.subtract).then_inc(wpm_ready, 1)


            def scatter(i):
                pool.wait_ge(slot_ready, i + 1)
                pool.sem_inc(slot_seen, 1)
                for t in range(TB):
                    pool.indirect_dma_start(
                        out=pair_slots, out_offset=bass.IndirectOffsetOnAxis(ap=slot[:, 0, t:t + 1], axis=0),
                        in_=tok[:, 1, t:t + 1], in_offset=None).then_inc(scattered, 16)
            pool.wait_ge(far_stored, 16)
            scatter(0)
            with pool.Fori(1, R - 1) as i:
                scatter(i)
            scatter(R - 1)
            pool.wait_ge(scattered, 16 * T)
            pool.wait_ge(rows_ready, 1)
            for h in range(2):
                pool.indirect_dma_start(out=tokT[:, h], out_offset=None, in_=pair_tokens,
                                        in_offset=bass.IndirectOffsetOnAxis(ap=trow[:, h:h + 1], axis=0)).then_inc(rows_loaded, 16)
            G.memset(arena[:, 11 * E:11 * E + U * INFO_W], 0.0).then_inc(inf_init, 1)
            pool.wait_ge(inf_init, 1)
            pool.wait_ge(info_stored, 16 * R)

            def gather(k):
                tokens = bass.IndirectOffsetOnAxis(ap=gidx[:, k:k + 1], axis=0)
                pool.indirect_dma_start(out=x2[:, k], out_offset=None, in_=x_rows, in_offset=tokens,
                                        bounds_check=N - 1, oob_is_err=False).then_inc(ld_x2[k], 16)
                pool.indirect_dma_start(out=inf2[:, k], out_offset=None, in_=info_dram, in_offset=tokens,
                                        bounds_check=N - 1, oob_is_err=False).then_inc(ld_x2[k], 16)

            def scatter_out(k):
                pool.indirect_dma_start(out=out_rows, out_offset=bass.IndirectOffsetOnAxis(ap=sidx[:, k:k + 1], axis=0),
                                        in_=o2[:, k % 2], in_offset=None,
                                        bounds_check=N - 1, oob_is_err=False).then_inc(stored[k % 2], 16)

            def step(i, k, last=False):
                j, b = i * U + k, k % 2
                pool.wait_ge(sg_ready, j + 1)
                after(pool, stored[b], 16 * (i * (U // 2) + k // 2))
                G.tensor_tensor(o2[:, b], sg2[:, b], x2[:, k], ALU.add).then_inc(o_ready, 1)
                pool.wait_ge(sidx_ready, j + 1)
                if not last:
                    pool.wait_ge(gidx_ready, j + U + 1)
                pool.wait_ge(o_ready, j + 1)
                pool.sem_inc(o_seen, 1)
                if not last:
                    gather(k)
                scatter_out(k)
            for k in range(U):
                pool.wait_ge(gidx_ready, k + 1)
                gather(k)
            rounds(pool, NT // U, step)
            for b in range(2):
                pool.wait_ge(stored[b], 16 * (NT // 2))

        @block.scalar
        def _(act):
            act.wait_ge(d_ready, 1)
            nc.scalar.activation(v["sd"], v["ve"], ACT.Sqrt).then_inc(act_setup, 1)
            act.wait_ge(d_ready, 2)
            nc.scalar.activation(v["ly"], v["cnt"], ACT.Ln).then_inc(act_setup, 1)
            act.wait_ge(d_ready, 3)
            nc.scalar.activation(v["s1"], v["arg"], ACT.Sin, scale=0.5)
            nc.scalar.activation(v["q1"], v["arg"], ACT.Sin, scale=0.25)
            nc.scalar.activation(v["q2"], v["ph"], ACT.Sin, scale=0.5).then_inc(act_setup, 1)
            for s in range(2):
                act.wait_ge(c_mm, s + 1)
                cps = psum[:, s].rearrange("p (k h) -> p k h", k=CH)
                nc.scalar.activation(cf[:, s], cps, ACT.Copy)
                nc.scalar.activation(c_hi[:, s], cps, ACT.Copy).then_inc(c_copied, 1)
            act.wait_ge(m_mm, 1)
            nc.scalar.activation(msb, psum[:, 2, 0:C * GOLAY_N].rearrange("p (c n) -> p c n", c=C), ACT.Copy,
                                 scale=1.0 / CS).then_inc(m_copied, 1)
            act.wait_ge(rt_mm, 1)
            nc.scalar.activation(wcat[:, :, 0:NE], psum[:, 3, 0:C * NE].rearrange("p (c n) -> p c n", c=C),
                                 ACT.Copy).then_inc(m_copied, 1)
            for e in range(NE):
                act.wait_ge(wscale_ready, e // LH + 1)
                act.wait_ge(wpm_ready, e + 1)
                nc.scalar.activation(w_hi[:, e], wpm[:, e % 2], ACT.Copy, scale=wscale[:, e:e + 1]).then_inc(whi_ready, 1)

            def turn_copy(i, k, q):
                t = (i * U + k) * GT + q
                act.wait_ge(t1_done, t + 1)
                if q == 0:
                    after(act, mm1_done, i * U + k - 1)
                nc.scalar.activation(xT4[:, k % 2, :, q * P:(q + 1) * P], psum[:, q % 2].rearrange("p (c n) -> p c n", c=C),
                                     ACT.Copy).then_inc(t1_copied, 1)

            def latT_copy(i, k):
                g = i * U + k
                act.wait_ge(mm1_done, g + 1)
                after(act, back_done, g - 1)
                nc.scalar.activation(latT[:, k % 2], psum[:, 2], ACT.Copy).then_inc(latT_copied, 1)

            def exps(n):
                act.wait_ge(dx_ready, n + 1)
                nc.scalar.activation(ex, dl, ACT.Exp)
                nc.scalar.activation(e2, d2, ACT.Exp).then_inc(exp_ready, 1)

            def bits_copy(n):
                act.wait_ge(corr_ready, n + 1)
                after(act, info_stored, 16 * n)
                for c in range(3):
                    last = nc.scalar.activation(info_bits[:, :, c, 0:GOLAY_N], bits.rearrange("p n t -> p t n"), ACT.Copy)
                last.then_inc(bits_copied, 1)

            def info_store(n):
                act.wait_ge(info_ready, n + 1)
                act.wait_ge(bits_copied, n + 1)
                act.dma_start(info_tiles[:, bass.ds(n * TB, TB), :], info[:, :, :]).then_inc(info_stored, 16)

            def step1(i, k, last=False):
                ahead = not (last and k + 1 >= U)
                if later_than_first(i) and k == 1:
                    exps(i - 1)
                if ahead:
                    turn_copy(*at(i, k, 1), 0)
                latT_copy(i, k)
                if later_than_first(i) and k == 1:
                    bits_copy(i - 1)
                if ahead:
                    for q in range(1, GT):
                        turn_copy(*at(i, k, 1), q)
                if k == 2:
                    act.wait_ge(var_ready, i + 1)
                    nc.scalar.activation(rt1[:, 1], rt1[:, 0], ACT.Sqrt).then_inc(sd_ready, 1)
                if later_than_first(i) and k == 3:
                    info_store(i - 1)
            act.wait_ge(far_stored, 16)
            act.wait_ge(info_init, 1)
            for q in range(GT):
                turn_copy(0, 0, q)
            rounds(act, R, step1, head=2)
            exps(R - 1)
            bits_copy(R - 1)
            info_store(R - 1)

            def front(i, k):
                j, b = i * U + k, k % 2
                act.wait_ge(uvT_done, j + 1)
                after(act, y_done, j - 1)
                nc.scalar.activation(hl2[:, b], psum[:, 0].bitcast(F16).rearrange("p (v c n) -> p v c n", v=2, c=C), ACT.Copy)
                nc.scalar.activation(bT2[:, b], psum[0:96, 1, 0:P // 2].bitcast(BF16), ACT.Copy).then_inc(hl_ready, 1)

            def step(i, k, last=False):
                j, b = i * U + k, k % 2
                act.wait_ge(e_done, 2 * j + 1)
                after(act, z_ready, j - 1)
                nc.scalar.activation(t2[:, b], psum[:, 4 + b], ACT.Identity, scale=inf2[:, k, 3:4],
                                     bias=inf2[:, k, 2:3]).then_inc(t_ready, 1)
                if not (last and k + 1 >= U):
                    front(*at(i, k, 1))
                act.wait_ge(z_ready, j + 1)
                after(act, sg_ready, j - 1)
                nc.scalar.activation(g2[:, b], z2[:, b], ACT.Silu).then_inc(g_ready, 1)
                act.wait_ge(y_done, j + 1)
                after(act, s_ready, j - 1)
                nc.scalar.activation(ysb2[:, b, 0:H], psum[:, 2 + b, H:E], ACT.Copy, scale=1.0 / (XS * CS)).then_inc(y_copied, 1)
            front(0, 0)
            rounds(act, NT // U, step)

        @block.vector
        def _(dve):
            n = [0]

            def link(ins):
                n[0] += 1
                ins.then_inc(dch, 1)
                dve.wait_ge(dch, n[0])

            def chain(s, base):
                c = [0]

                def link_in(ins):
                    c[0] += 1
                    ins.then_inc(s, 1)
                    dve.wait_ge(s, base + c[0])
                return link_in
            V = nc.vector
            dve.wait_ge(ld_x01, 16)
            for r in range(2):
                last = V.bn_stats(v["st"][:, r], x01[:, r * E:(r + 1) * E])
            link(last)
            for r in range(2):
                last = V.bn_aggr(v["mv"][:, r], v["st"][:, r])
            link(last)
            V.tensor_scalar(v["ve"], v["mv"][:, :, 1], EPS, None, ALU.add).then_inc(d_ready, 1)
            dve.wait_ge(act_setup, 1)
            link(V.reciprocal(v["r0"], v["sd"]))
            link(V.tensor_tensor(v["rt"], v["r0"], v["r0"], ALU.mult))
            link(V.tensor_tensor(v["rt"], v["rt"], v["ve"], ALU.mult))
            link(V.tensor_scalar(v["rt"], v["rt"], -0.5, 1.5, ALU.mult, ALU.add))
            link(V.tensor_tensor(v["r0"], v["r0"], v["rt"], ALU.mult))
            for r in range(2):
                last = V.tensor_scalar(junk[:, r * E:(r + 1) * E], x01[:, r * E:(r + 1) * E], v["mv"][:, r, 0:1],
                                       v["r0"][:, r:r + 1], ALU.subtract, ALU.mult)
            link(last)
            for c, side in enumerate(BLOCKS):
                last = V.tensor_reduce(v["mu"][:, c:c + 1], junk[:, 0:side * side], AXX, ALU.add)
            link(last)
            for c, side in enumerate(BLOCKS):
                last = V.tensor_scalar(v["mu"][:, c:c + 1], v["mu"][:, c:c + 1], 1.0 / (side * side), None, ALU.mult)
            link(last)
            for c, side in enumerate(BLOCKS):
                link(V.tensor_scalar(x01[:, 0:side * side], junk[:, 0:side * side], v["mu"][:, c:c + 1], 0.0, ALU.is_gt,
                                     ALU.add, accum_out=v["cnt"][:, c:c + 1]))
            V.tensor_scalar(v["cnt"], v["cnt"], 1.0, None, ALU.max).then_inc(d_ready, 1)
            dve.wait_ge(ld_cst, 16)
            dve.wait_ge(act_setup, 2)
            link(V.tensor_tensor(v["ly"], v["ly"], slope_c, ALU.mult))
            link(V.tensor_reduce(v["D"], v["ly"], AXX, ALU.add))
            link(V.tensor_scalar(v["D"], v["D"], 1.0, 2.0, ALU.max, ALU.min))
            V.tensor_scalar(v["wD"], v["D"], 0.2, 1.0, ALU.mult, ALU.add)
            V.tensor_scalar(v["a"], v["D"], 0.5, 1.0, ALU.mult, ALU.add)
            V.tensor_scalar(v["b"], v["D"], 0.1, None, ALU.mult)
            link(V.tensor_tensor(v["ph"], ka, ka, ALU.mult))
            link(V.tensor_tensor(v["wD"], v["wD"], v["D"], ALU.mult))
            V.tensor_scalar(v["arg"], ka, v["a"], v["wD"], ALU.mult, ALU.add)
            link(V.scalar_tensor_tensor(v["ph"], v["ph"], v["b"], ka, ALU.mult, ALU.subtract))
            V.tensor_scalar(v["ph"], v["ph"], v["wD"], None, ALU.add).then_inc(d_ready, 1)
            dve.wait_ge(act_setup, 3)
            V.tensor_tensor(v["q1"], v["q1"], v["q1"], ALU.mult)
            link(V.tensor_tensor(v["q2"], v["q2"], v["q2"], ALU.mult))
            V.tensor_scalar(v["q1"], v["q1"], -2.0, 1.0, ALU.mult, ALU.add)
            link(V.tensor_scalar(v["q2"], v["q2"], -2.0, 1.0, ALU.mult, ALU.add))
            link(V.tensor_tensor(v["q1"], v["q1"], v["q2"], ALU.mult))
            link(V.tensor_tensor(v["q1"], v["q1"], v["s1"], ALU.mult))
            link(V.tensor_tensor(v["q1"], v["q1"], kw, ALU.mult))
            for c in range(C):
                last = V.tensor_scalar(tabf[:, c], tab[:, c], v["q1"][:, c:c + 1], 2.0 * CS, ALU.mult, ALU.mult)
            last.then_inc(filt_ready, 1)
            dve.wait_ge(ld_small, 16 * 8)
            V.tensor_tensor(welpm[:, 0:CH], welraw[:, 0:CH], welraw[:, CH:C], ALU.add)
            V.tensor_tensor(welpm[:, CH:C], welraw[:, 0:CH], welraw[:, CH:C], ALU.subtract).then_inc(wel_ready, 1)
            V.tensor_scalar(bel[:, :], bel[:, :], -1.0, None, ALU.mult)
            V.tensor_tensor(wlpm[:, 0:H], wle[:, 0:H], wle[:, H:E], ALU.add)
            link(V.tensor_tensor(wlpm[:, H:E], wle[:, 0:H], wle[:, H:E], ALU.subtract))
            half = XS * CS / 2
            link(V.tensor_scalar(wlh, wlpm, half, None, ALU.mult))
            link(V.scalar_tensor_tensor(wlr, wlpm, half, wlh, ALU.mult, ALU.subtract))
            link(V.tensor_copy(wlm, wlr))
            V.tensor_copy(wle3[0:32], wlh[0:32])
            V.tensor_copy(wle3[32:64], wlm[32:64])
            V.tensor_tensor(wle3[64:96], wlr[64:96], wlm[64:96], ALU.subtract).then_inc(wle_ready, 1)
            for s in range(2):
                dve.wait_ge(c_copied, s + 1)
                V.tensor_tensor(c_lo[:, s], psum[:, s].rearrange("p (k h) -> p k h", k=CH), c_hi[:, s],
                                ALU.subtract).then_inc(c_lo_ready, 1)
            V.tensor_copy(nbefore[:, :], nbefore_c)
            V.tensor_copy(used[:, :], region_c).then_inc(sort_init, 1)
            dve.wait_ge(iota_ready, 1)
            link(V.tensor_copy(tokf[:, :], tok[:, 0, :]))
            dve.wait_ge(m_copied, 2)
            dve.wait_ge(zeroed, 2)
            V.tensor_tensor(wcat[:, 0:CH, NE:NL], msb[:, 0:CH], msb[:, CH:C], ALU.add)
            V.tensor_tensor(wcat[:, CH:C, NE:NL], msb[:, 0:CH], msb[:, CH:C], ALU.subtract).then_inc(wcat_raw, 1)
            dve.wait_ge(wmean_mm, 1)
            V.tensor_tensor(wcat[:, :, 0:NL], wcat[:, :, 0:NL], psum[:, 4, 0:NL].unsqueeze(1).broadcast_to([P, C, NL]),
                            ALU.subtract).then_inc(wcat_ready, 1)

            for half_no in range(NE // LH):
                for e in range(LH * half_no, LH * half_no + LH):
                    dve.wait_ge(ld_w[e % LH], 16 * (half_no + 1))
                    V.tensor_reduce(amax[:, e:e + 1], raw[:, e % LH].rearrange("p c e -> p (c e)"), AXX, ALU.max,
                                    apply_absolute_value=True).then_inc(amax_ready, 1)
                dve.wait_ge(amax_red, half_no + 1)
                hs = slice(LH * half_no, LH * half_no + LH)
                link(V.tensor_scalar(amax_all[:, hs], amax_all[:, hs], 1e-25, None, ALU.max))
                link(V.reciprocal(wscale[:, hs], amax_all[:, hs]))
                V.tensor_scalar(unscale[:, hs], amax_all[:, hs], 0.5 / (XS * WS), None, ALU.mult)
                ins = V.tensor_scalar(wscale[:, hs], wscale[:, hs], WS, None, ALU.mult)
                ins.then_inc(wscale_ready, 1)
                dve.wait_ge(wscale_ready, half_no + 1)
                for e in range(LH * half_no, LH * half_no + LH):
                    dve.wait_ge(whi_ready, e + 1)
                    V.scalar_tensor_tensor(w_lo[:, e], wpm[:, e % 2], wscale[:, e:e + 1], w_hi[:, e], ALU.mult,
                                           ALU.subtract).then_inc(wlo_ready, 1)

            def stats(i, k):
                dve.wait_ge(ld_x[k], 16 * (i + 1))
                for q in range(GT):
                    last = V.bn_stats(st6[:, k * GT + q], xbuf[:, k, q])
                last.then_inc(stats_ready, 1)

            def deviations(i):
                dve.wait_ge(stats_ready, U * (i + 1))
                V.tensor_copy(rt1[:, 3], st6[:, :, 0])
                for t in range(TB):
                    last = V.bn_aggr(mv1[:, t], st6[:, t])
                last.then_inc(aggr_ready, 1)
                dve.wait_ge(aggr_ready, i + 1)
                V.tensor_scalar(rt1[:, 0], mv1[:, :, 1], EPS, None, ALU.add).then_inc(var_ready, 1)
                V.tensor_scalar(mean2[:, :], mv1[:, :, 0], 2.0, None, ALU.mult)

            def inverse_root(i):
                ve, sd, r0, rt = (rt1[:, c] for c in range(4))
                link_n = chain(newton, 4 * i)
                dve.wait_ge(sd_ready, i + 1)
                link_n(V.reciprocal(r0, sd))
                link_n(V.tensor_tensor(rt, r0, r0, ALU.mult))
                link_n(V.tensor_tensor(rt, rt, ve, ALU.mult))
                link_n(V.tensor_scalar(rt, rt, -0.5, 1.5, ALU.mult, ALU.add))
                V.tensor_tensor(rstd[:, :], r0, rt, ALU.mult).then_inc(rstd_ready, 1)

            def over(a):
                return a.rearrange("p n t -> p t n")

            def each(a, m):
                return a.unsqueeze(1).broadcast_to([P, m, TB])

            def along(a, m):
                return a.unsqueeze(2).broadcast_to([P, m, TB])

            def choose(n):
                lk = chain(route_a, 12 * n)
                dve.wait_ge(rstd_ready, n + 1)
                dve.wait_ge(back_done, U * (n + 1))
                for h in range(2):
                    ts = slice(h * TB // 2, (h + 1) * TB // 2)
                    V.tensor_tensor(lat[:, :, ts], psum[:, 4 + h, 0:TB // 2 * NL].rearrange("p (t n) -> p n t", n=NL),
                                    rstd[:, ts].unsqueeze(1).broadcast_to([P, NL, TB // 2]), ALU.mult).then_inc(lat_copied, 1)
                dve.wait_ge(lat_copied, 2 * (n + 1))
                after(dve, bits_copied, n)
                V.tensor_tensor(bits[:, :, :], lat[:, NE:NL], along(bel[:, :], GOLAY_N), ALU.is_gt)
                lk(V.tensor_reduce(m1, over(lg), AXX, ALU.max))
                V.tensor_reduce(nlow, over(bits[:, 0:GOLAY_R]), AXX, ALU.add)
                V.tensor_reduce(nhigh, over(bits[:, GOLAY_R:]), AXX, ALU.add)
                lk(V.tensor_tensor(eq, lg, each(m1, NE), ALU.is_equal))
                V.scalar_tensor_tensor(fix, nlow, 4.0, nhigh, ALU.mult, ALU.add)
                lk(V.tensor_tensor(sc, eq, along(ramp, NE), ALU.mult))
                V.tensor_scalar(fix, fix, 3.0, None, ALU.is_le)
                lk(V.tensor_reduce(mx1, over(sc), AXX, ALU.max))
                V.tensor_tensor(fixadd[:, :, :], bits[:, GOLAY_R:], each(fix, GOLAY_R), ALU.mult)
                lk(V.tensor_tensor(oh1, sc, each(mx1, NE), ALU.is_equal))
                V.tensor_tensor(bits[:, 0:GOLAY_R], bits[:, 0:GOLAY_R], fixadd[:, :, :], ALU.add).then_inc(corr_ready, 1)
                lk(V.scalar_tensor_tensor(l2, oh1, -3e38, lg, ALU.mult, ALU.add))
                V.tensor_tensor(dl, lg, each(m1, NE), ALU.subtract)
                lk(V.tensor_reduce(m2, over(l2), AXX, ALU.max))
                V.tensor_tensor(d2, m2, m1, ALU.subtract).then_inc(dx_ready, 1)
                lk(V.tensor_tensor(eq, l2, each(m2, NE), ALU.is_equal))
                lk(V.tensor_tensor(sc, eq, along(ramp, NE), ALU.mult))
                lk(V.tensor_reduce(mx2, over(sc), AXX, ALU.max))
                V.tensor_tensor(oh2, sc, each(mx2, NE), ALU.is_equal)
                V.tensor_tensor(kmin, mx1, mx2, ALU.min)
                V.tensor_tensor(isa, mx1, mx2, ALU.is_gt)
                lk(V.tensor_tensor(kmax, mx1, mx2, ALU.max))
                V.tensor_scalar(isb, isa, -1.0, 1.0, ALU.mult, ALU.add)
                lk(V.scalar_tensor_tensor(kmax, kmax, float(NE), kmin, ALU.mult, ALU.add))
                V.tensor_tensor(pairs[:, :, :], each(kmax, NQ), along(key_c, NQ), ALU.is_equal).then_inc(pairs_ready, 1)

            def weigh(n):
                lk = chain(route_c, 11 * n)
                uns = along(unscale[:, :], NE)
                dve.wait_ge(exp_ready, n + 1)
                V.tensor_reduce(zs, over(ex), AXX, ALU.add)
                lk(V.tensor_tensor(ux, oh1, uns, ALU.mult))
                V.tensor_reduce(u1, over(ux), AXX, ALU.add)
                lk(V.reciprocal(p1, zs))
                V.tensor_tensor(p2, e2, p1, ALU.mult)
                lk(V.tensor_tensor(ux, oh2, uns, ALU.mult))
                V.tensor_reduce(u2, over(ux), AXX, ALU.add)
                lk(V.tensor_tensor(den, p1, p2, ALU.add))
                lk(V.tensor_scalar(den, den, 1e-6, None, ALU.add))
                lk(V.reciprocal(den, den))
                V.tensor_tensor(w1, p1, den, ALU.mult)
                lk(V.tensor_tensor(w2, p2, den, ALU.mult))
                V.tensor_tensor(p1, p1, w1, ALU.mult)
                V.tensor_tensor(p2, p2, w2, ALU.mult)
                V.tensor_tensor(u1, u1, w1, ALU.mult)
                lk(V.tensor_tensor(u2, u2, w2, ALU.mult))
                after(dve, info_stored, 16 * n)
                V.tensor_tensor(info[:, :, 2], p1, p2, ALU.add)
                V.tensor_copy(info[:, :, 0], mean2[:, :])
                V.tensor_scalar(info[:, :, 1], rstd[:, :], XS, None, ALU.mult)
                V.tensor_tensor(wt1, isa, u1, ALU.mult)
                lk(V.tensor_tensor(wt2, isb, u2, ALU.mult))
                lk(V.tensor_tensor(info[:, :, 3], wt1, wt2, ALU.add))
                V.tensor_tensor(wt1, isb, u1, ALU.mult)
                lk(V.tensor_tensor(wt2, isa, u2, ALU.mult))
                V.tensor_tensor(info[:, :, 4], wt1, wt2, ALU.add).then_inc(info_ready, 1)

            def place(n):
                lk = chain(route_d, 5 * n)
                totals = psum[:, 7, 0:NQ * TB].rearrange("p (q t) -> p q t", q=NQ)
                within = psum[:, 6, 0:NQ * TB].rearrange("p (q t) -> p q t", q=NQ)
                dve.wait_ge(rank_mm, n + 1)
                V.tensor_scalar(tokf[:, :], tokf[:, :], float(P * TB), None, ALU.add)
                lk(V.tensor_tensor(totals[:, :, 0], totals[:, :, 0], used[:, :], ALU.add))
                lk(V.tensor_tensor_scan(ranks.rearrange("p q t -> p (q t)"), carry_c, psum[:, 7, 0:NQ * TB], 0.0,
                                        ALU.mult, ALU.add))
                V.tensor_copy(used[:, :], ranks[:, :, TB - 1])
                lk(V.tensor_tensor(slots[:, :, :], within, ranks[:, :, :], ALU.add))
                lk(V.tensor_tensor(slots[:, :, :], slots[:, :, :], pairs[:, :, :], ALU.mult))
                lk(V.tensor_reduce(slotf, over(slots), AXX, ALU.add))
                after(dve, scattered, 16 * TB * n)
                V.tensor_copy(tok[:, 1, :], tokf[:, :])
                V.tensor_copy(slot[:, 0, :], slotf).then_inc(slot_ready, 1)

            def step1(i, k, last=False):
                later = later_than_first(i)
                if not (last and k + 1 >= U):
                    stats(*at(i, k, 1))
                if later and k == 0:
                    choose(i - 1)
                if later and k == 2:
                    weigh(i - 1)
                if k == 2:
                    deviations(i)
                if later and k == 3:
                    place(i - 1)
                if k == 3:
                    inverse_root(i)
            dve.wait_ge(sort_init, 1)
            dve.wait_ge(info_init, 1)
            stats(0, 0)
            rounds(dve, R, step1, head=2)
            choose(R - 1)
            weigh(R - 1)
            place(R - 1)

            count, tiles, end = (tq[:, c] for c in range(3))
            dve.wait_ge(slot_ready, R)
            V.memset(tmul[:, 0], 1.0)
            V.memset(tcmp[:, :, NQ:NQ + 1], 0.0)
            link(V.tensor_tensor(count, used[:, :], region_c, ALU.subtract))
            link(V.tensor_scalar(tiles, count, 1.0 / P, (P - 1) / (2.0 * P), ALU.mult, ALU.add))
            link(V.tensor_scalar(tiles, tiles, 8388608.0, None, ALU.add))
            link(V.tensor_scalar(tiles, tiles, 8388608.0, None, ALU.subtract))
            link(V.tensor_tensor_scan(end, tmul[:, 0], tiles, 0.0, ALU.mult, ALU.add))
            link(V.tensor_tensor(end, end, tiles, ALU.subtract))
            V.tensor_tensor(count, row_c, end, ALU.subtract)
            link(V.tensor_tensor(tcmp[:, :, 0:NQ], tile_c.unsqueeze(2).broadcast_to([P, 2, NQ]),
                                 end.unsqueeze(1).broadcast_to([P, 2, NQ]), ALU.is_ge))
            link(V.tensor_tensor(tone[:, :, :], tcmp[:, :, 0:NQ], tcmp[:, :, 1:NQ + 1], ALU.subtract))
            for c, values in enumerate((first_c, second_c, count)):
                link(V.tensor_tensor(tmul[:, :, :], tone[:, :, :], values.unsqueeze(1).broadcast_to([P, 2, NQ]), ALU.mult))
                link(V.tensor_reduce(tval[:, c], tmul[:, :, :], AXX, ALU.add))
            V.tensor_tensor(trow[:, :], tval[:, 2], tile_c, ALU.add).then_inc(rows_ready, 1)
            dve.wait_ge(exps_mm, 1)
            V.tensor_copy(tile_exp[:, :, :], psum[0:1, 1, 0:4 * P].rearrange("o (v t) -> o v t", v=2)).then_inc(tiles_ready, 1)
            dve.wait_ge(rows_loaded, 32)
            V.tensor_copy(tokTf[:, :, :], tokT[:, :, :]).then_inc(rows_float, 1)
            dve.wait_ge(rows_turned, 1)
            V.tensor_copy(tile_tok[:, :], psum[:, 0, 0:2 * P]).then_inc(tiles_ready, 1)

            def gidx_copy(i, k):
                V.tensor_copy(gidx[:, k:k + 1], tile_tok[:, bass.ds(i * U + k, 1)]).then_inc(gidx_ready, 1)

            def split(i, k):
                j, b = i * U + k, k % 2
                dve.wait_ge(ld_x2[k], 32 * (i + 1))
                V.tensor_tensor(raw2[:, b, 0:H], x2[:, k, 0:H], x2[:, k, H:E], ALU.add).then_inc(raw_ready, 1)
                V.tensor_tensor(uv2[:, b, H:E], x2[:, k, 0:H], x2[:, k, H:E], ALU.subtract)
                dve.wait_ge(raw_ready, j + 1)
                V.tensor_scalar(uv2[:, b, 0:H], raw2[:, b, 0:H], inf2[:, k, 0:1], None, ALU.subtract).then_inc(uv_ready, 1)
                dve.wait_ge(uv_ready, j + 1)
                after(dve, uvT_done, j - 1)
                V.tensor_scalar(hi2[:, b], uv2[:, b], inf2[:, k, 1:2], None, ALU.mult).then_inc(hi_ready, 1)
                dve.wait_ge(hi_ready, j + 1)
                V.scalar_tensor_tensor(lo2[:, b], uv2[:, b], inf2[:, k, 1:2], hi2[:, b], ALU.mult,
                                       ALU.subtract).then_inc(split_ready, 1)

            def step(i, k, last=False):
                j, b = i * U + k, k % 2
                dve.wait_ge(t_ready, j + 1)
                after(dve, g_ready, j - 1)
                dve.wait_ge(e_done, 2 * j + 2)
                V.scalar_tensor_tensor(z2[:, b], psum[:, 6 + b], inf2[:, k, 4:5], t2[:, b], ALU.mult,
                                       ALU.add).then_inc(z_ready, 1)
                if not (last and k + 2 >= U):
                    split(*at(i, k, 2))
                if not last:
                    gidx_copy(i + 1, k)
                if later_than_first(i):
                    dve.wait_ge(stored[b], 16 * ((i - 1) * (U // 2) + k // 2 + 1))
                dve.wait_ge(y_copied, j + 1)
                for half, sign in enumerate((ALU.add, ALU.subtract)):
                    ins = V.scalar_tensor_tensor(s2[:, b, half * H:(half + 1) * H], psum[:, 2 + b, 0:H], 1.0 / (XS * CS),
                                                 ysb2[:, b, 0:H], ALU.mult, sign)
                ins.then_inc(s_ready, 1)
                V.tensor_copy(sidx[:, k:k + 1], tile_tok[:, bass.ds(j, 1)]).then_inc(sidx_ready, 1)
                after(dve, o_ready, j - 1)
                dve.wait_ge(g_ready, j + 1)
                dve.wait_ge(s_ready, j + 1)
                V.tensor_tensor(sg2[:, b], s2[:, b], g2[:, b], ALU.mult).then_inc(sg_ready, 1)
            dve.wait_ge(tiles_ready, 2)
            for k in range(U):
                gidx_copy(0, k)
            split(0, 0)
            split(0, 1)
            rounds(dve, NT // U, step)

        @block.tensor
        def _(pe):
            mm = nc.tensor.matmul
            pe.wait_ge(ident_ready, 2)
            pe.wait_ge(ld_router, 16)
            for c in range(C):
                last = nc.tensor.transpose(psum[:, 3, c * NE:(c + 1) * NE], rtr[:, c * P:(c + 1) * P], ident[0:NE, 0:NE])
            last.then_inc(rt_mm, 1)
            pe.wait_ge(filt_ready, 1)
            for s in range(2):
                for ih in range(CH):
                    for kc in range(CH):
                        last = nc.tensor.matmul(psum[:, s, ih * H:(ih + 1) * H], tabf[:, 2 * s + kc, ih * P:(ih + 1) * P],
                                                tab[:, 2 * s + kc], start=(kc == 0), stop=(kc == CH - 1))
                last.then_inc(c_mm, 1)
            pe.wait_ge(wel_ready, 1)
            for s in range(2):
                pe.wait_ge(c_copied, s + 1)
                for ih in range(CH):
                    m = 2 * s + ih
                    for kc in range(CH):
                        last = nc.tensor.matmul(psum[:, 2, m * GOLAY_N:(m + 1) * GOLAY_N], cf[:, s, kc, ih * P:(ih + 1) * P],
                                                welpm[:, 2 * s + kc], start=(kc == 0), stop=(kc == CH - 1))
            last.then_inc(m_mm, 1)

            pe.wait_ge(wcat_raw, 1)
            pe.wait_ge(ones_ready, 1)
            for c in range(C):
                last = nc.tensor.matmul(psum[:, 4, 0:NL], avg[:, :], wcat[:, c, 0:NL], start=(c == 0), stop=(c == C - 1))
            last.then_inc(wmean_mm, 1)

            pe.wait_ge(c_lo_ready, 2)
            pe.wait_ge(wcat_ready, 1)

            def turn(i, k, q):
                t = (i * U + k) * GT + q
                if q == 0:
                    pe.wait_ge(ld_x[k], 16 * (i + 1))
                after(pe, t1_copied, t - 1)
                for c in range(C):
                    last = nc.tensor.transpose(psum[:, q % 2, c * P:(c + 1) * P], xbuf[:, k, q, c * P:(c + 1) * P], ident[:, :])
                last.then_inc(t1_done, 1)

            def logits(i, k):
                g = i * U + k
                pe.wait_ge(t1_copied, GT * (g + 1))
                after(pe, latT_copied, g)
                for c in range(C):
                    last = mm(psum[:, 2], wcat[:, c], xT4[:, k % 2, c], start=(c == 0), stop=(c == C - 1))
                last.then_inc(mm1_done, 1)

            def turn_back(i, k):
                pe.wait_ge(latT_copied, i * U + k + 1)
                after(pe, lat_copied, 2 * i)
                pe.sem_inc(latT_seen, 1)
                for q in range(GT):
                    t = k * GT + q
                    col = t % (TB // 2) * NL
                    last = nc.tensor.transpose(psum[:, 4 + t // (TB // 2), col:col + NL], latT[0:NL, k % 2, q * P:(q + 1) * P],
                                               ident[0:NL, 0:NL])
                last.then_inc(back_done, 1)

            def rank(n):
                pe.wait_ge(pairs_ready, n + 1)
                onehot = pairs.rearrange("p q t -> p (q t)")
                mm(psum[:, 6, 0:NQ * TB], nbefore[:, :], onehot, start=True, stop=True)
                mm(psum[:, 7, 0:NQ * TB], ones[:, :], onehot, start=True, stop=True).then_inc(rank_mm, 1)

            def step1(i, k, last=False):
                ahead = not (last and k + 1 >= U)
                nxt = at(i, k, 1)
                if ahead:
                    turn(*nxt, 0)
                logits(i, k)
                if ahead:
                    turn(*nxt, 1)
                    turn(*nxt, 2)
                turn_back(i, k)
                if ahead:
                    turn(*nxt, 3)
                if later_than_first(i) and k == 2:
                    rank(i - 1)
            pe.wait_ge(sort_init, 1)
            for q in range(GT):
                turn(0, 0, q)
            rounds(pe, R, step1)
            rank(R - 1)

            pe.wait_ge(rows_ready, 1)
            pe.wait_ge(t1_copied, T)
            for c in range(2):
                for h in range(2):
                    last = mm(psum[0:1, 1, (2 * c + h) * P:(2 * c + h + 1) * P], tval[:, c, h:h + 1], ident[:, :],
                              start=True, stop=True)
            last.then_inc(exps_mm, 1)
            pe.wait_ge(rows_float, 1)
            for h in range(2):
                last = nc.tensor.transpose(psum[:, 0, h * P:(h + 1) * P], tokTf[:, h], ident[:, :])
            last.then_inc(rows_turned, 1)

            pe.wait_ge(tiles_ready, 2)
            pe.wait_ge(wlo_ready, NE)

            def front(i, k):
                j, b = i * U + k, k % 2
                pe.wait_ge(split_ready, j + 1)
                after(pe, hl_ready, j)
                nc.tensor.transpose(psum[0:96, 1, 0:P // 2].bitcast(BF16), inf2[:, k, 16:64].bitcast(BF16), ident_b[:, :])
                turned = psum[:, 0].bitcast(F16).rearrange("p (v c n) -> p v c n", v=2, c=C)
                for v_, part in enumerate((hi2, lo2)):
                    for c in range(C):
                        last = nc.tensor.transpose(turned[:, v_, c], part[:, b, c * P:(c + 1) * P], ident_h[:, :])
                last.then_inc(uvT_done, 1)

            def step(i, k, last=False):
                j, b = i * U + k, k % 2
                which = [pe.value_load(tile_exp[0:1, c, bass.ds(j, 1)], min_val=0, max_val=NE - 1) for c in range(2)]
                hi, lo = hl2[:, b, 0], hl2[:, b, 1]

                def expert(c_, e):
                    ps = psum[:, 4 + 2 * c_ + b]
                    for c in range(C):
                        wh = w_hi[:, bass.ds(e, 1), c].rearrange("p o n -> p (o n)")
                        wl = w_lo[:, bass.ds(e, 1), c].rearrange("p o n -> p (o n)")
                        mm(ps, hi[:, c], wh, start=(c == 0), stop=False)
                        mm(ps, hi[:, c], wl, start=False, stop=False)
                        end = mm(ps, lo[:, c], wh, start=False, stop=(c == C - 1))
                    end.then_inc(e_done, 1)
                after(pe, t_ready, j - 1)
                pe.wait_ge(hl_ready, j + 1)
                expert(0, which[0])
                if not (last and k + 1 >= U):
                    front(*at(i, k, 1))
                after(pe, z_ready, j - 1)
                expert(1, which[1])
                after(pe, s_ready, j - 1)
                yb = psum[:, 2 + b]
                mm(yb, bT2[:, b], wle3[:, :], start=True, stop=False)
                for s in range(2):
                    ys = yb[:, s * H:(s + 1) * H]
                    for kc in range(CH):
                        c = s * CH + kc
                        mm(ys, hi[:, c], c_hi[:, s, kc], start=False, stop=False)
                        mm(ys, hi[:, c], c_lo[:, s, kc], start=False, stop=False)
                        end = mm(ys, lo[:, c], c_hi[:, s, kc], start=False, stop=(s == 1 and kc == CH - 1))
                end.then_inc(y_done, 1)
            front(0, 0)
            rounds(pe, NT // U, step)


_INS = ["L0_attn_x", "L0_attn_W_el", "L0_attn_b_el", "L0_attn_W_le", "L0_attn_b_le", "L0_ffn_router_w",
        "L0_ffn_expert_weights"]


def kernel(**inputs):
    import concourse.bacc as bacc
    from concourse.bass_utils import run_bass_kernel_spmd as run

    nc = bacc.Bacc("TRN2", target_bir_lowering=False, num_devices=1)
    arrays, args = {}, []
    for name in _INS:
        a = np.ascontiguousarray(inputs[name])
        arrays[f"in_{name}"] = a
        args.append(nc.dram_tensor(f"in_{name}", a.shape, mybir.dt.from_np(a.dtype), kind="ExternalInput").ap())
    shape = arrays["in_L0_attn_x"].shape
    experts = arrays["in_L0_ffn_expert_weights"].shape[0]
    table = np.ascontiguousarray(np.concatenate([fourier_constants(shape[-1]), routing_constants(
        experts, shape[0] * shape[1], U * GT)], axis=1), dtype=np.float32)
    arrays["in_consts"] = table
    args.append(nc.dram_tensor("in_consts", table.shape, F32, kind="ExternalInput").ap())
    args.append(nc.dram_tensor("out_0", shape, F32, kind="ExternalOutput").ap())
    build(nc, *args)
    r = run(nc, [arrays], core_ids=[0])
    return r.results[0]["out_0"]
```

```python
import math
from contextlib import ExitStack

import numpy as np
import concourse.bass as bass
from concourse import mybir

F32 = mybir.dt.float32
F16 = mybir.dt.float16
I32 = mybir.dt.int32
BF16 = mybir.dt.bfloat16
ALU = mybir.AluOpType
ACT = mybir.ActivationFunctionType
AXX = mybir.AxisListType.X
RMAX = bass.bass_isa.ReduceOp.max

P = 128
HALVES = 2
GOLAY_N, GOLAY_R = 24, 12
XS = 1024.0
CS = 16384.0
WS = 16384.0
EPS = 1e-5
INFO_W = 64
GT = 4
U = 4
FAR = 1 << 20
BLOCKS = (2, 4, 8, 16, 32)


def fourier_constants(E):
    H = E // 2
    n = np.arange(H)
    rows, freq, weight = [], [], []
    for odd in (0, 1):
        ks = np.arange(odd, H + 1, 2)
        for kind in (np.cos, np.sin):
            for k in ks:
                if kind is np.sin and k in (0, H):
                    continue
                rows.append(kind(2 * np.pi * ((k * n) % E) / E))
                freq.append(k / E)
                weight.append((1.0 if k in (0, H) else 2.0) / E)
    C = E // P
    table = np.asarray(rows).reshape(C, P, H).transpose(1, 0, 2).reshape(P, C * H)
    ka = np.float32(np.asarray(freq, np.float32) + np.float32(1e-8)).reshape(C, P).T
    w = np.asarray(weight).reshape(C, P).T
    lx = np.log(np.asarray(BLOCKS, np.float64))
    n = len(BLOCKS)
    slope = -(n * lx - lx.sum()) / (n * (lx * lx).sum() - lx.sum() ** 2)
    return np.concatenate([table, ka, w, np.broadcast_to(slope, (P, n))], axis=1)


def routing_constants(NE, cap, TB):
    pairs = [(a, b) for a in range(NE) for b in range(a + 1, NE)]
    first, second = np.asarray(pairs).T
    q = np.arange(len(pairs))
    ramp = NE - np.arange(NE)
    key = NE * (NE - first) + (NE - second)
    region = q * cap
    carry = np.tile(np.arange(TB) > 0, len(pairs))
    tile = np.arange(P)[:, None] + P * np.arange(2)[None, :]
    not_before = -(np.arange(P)[:, None] >= np.arange(P)[None, :]).astype(np.float64)
    same = np.concatenate([ramp, key, first, second, region, region // P, carry])
    return np.concatenate([np.broadcast_to(same, (P, same.size)), tile, not_before], axis=1)


def build(nc, x_in, W_el, b_el, W_le, b_le, router_w, experts, consts, out):
    B, S, E = x_in.shape
    NE = experts.shape[0]
    N = B * S
    T = N // P
    C = E // P
    H = E // 2
    CH = H // P
    Q = H // 2
    TB = U * GT
    R = T // TB
    assert R == NE and Q == P
    NL = NE + GOLAY_N
    LH = 4
    NQ = NE * (NE - 1) // 2
    NT = -(-(T + NQ - 1) // U) * U
    TROWS = NQ * T + 2 * P

    x_rows = x_in.rearrange("b s e -> (b s) e")
    out_rows = out.rearrange("b s e -> (b s) e")
    x_tiles = x_rows.rearrange("(t p) e -> p t e", p=P)
    expert_rows = experts.rearrange("e (c p) n -> p e c n", p=P)
    info_dram = nc.dram_tensor("token_info", (N, INFO_W), F32, kind="Internal").ap()
    info_tiles = info_dram.rearrange("(t p) w -> p t w", p=P)
    pair_tokens = nc.dram_tensor("pair_tokens", (TROWS, P), I32, kind="Internal").ap()
    pair_slots = pair_tokens.rearrange("r (c o) -> (r c) o", o=1)

    ctx = ExitStack()
    with ctx:
        def sb(name, shape, dt=F32):
            return ctx.enter_context(nc.sbuf_tensor(name, shape, dt))

        def sem(name):
            return ctx.enter_context(nc.semaphore(name))

        w_hi = sb("w_hi", [P, NE, C, E], F16)
        w_lo = sb("w_lo", [P, NE, C, E], F16)
        arena = sb("arena", [P, 12288])
        xbuf = sb("xbuf", [P, U, GT, E])
        xT4 = sb("xT4", [P, 2, C, GT * P])
        CW = NE + 5 * NQ + NQ * TB + 2 + P
        cst = sb("cst", [P, C * H + 2 * C + len(BLOCKS) + CW])
        cq_hi = sb("cq_hi", [P, 2, Q], F16)
        cq_lo = sb("cq_lo", [P, 2, Q], F16)
        c_hi = sb("c_hi", [P, CH, H], F16)
        c_lo = sb("c_lo", [P, CH, H], F16)
        wle3 = sb("wle3", [96, E], BF16)
        ident = sb("ident", [P, P])
        ident_b = sb("ident_b", [P, P], BF16)
        ident_h = sb("ident_h", [P, P], F16)
        wcat = sb("wcat", [P, C, P])
        avg = sb("avg", [P, P])
        norm2 = sb("norm2", [P, NE])
        norm_all = sb("norm_all", [P, NE])
        wscale = sb("wscale", [P, NE, 2])
        wsc = sb("wsc", [P, 1, 2])
        unscale = sb("unscale", [P, NE])
        bel = sb("bel", [P, GOLAY_N])
        info = sb("info", [P, TB, INFO_W])
        lat = sb("lat", [P, NL, TB])
        latT = sb("latT", [P, 2, GT * P])
        st6 = sb("st6", [P, TB, 6])
        mv1 = sb("mv1", [P, TB, 2])
        rt1 = sb("rt1", [P, 4, TB])
        rstd = sb("rstd", [P, TB])
        mean4 = sb("mean4", [P, TB])
        rsc = sb("rsc", [P, 8, NE, TB])
        rsm = sb("rsm", [P, 26, TB])
        bits = sb("bits", [P, GOLAY_N, TB])
        fixadd = sb("fixadd", [P, GOLAY_R, TB])
        pairs = sb("pairs", [P, NQ, TB], F16)
        ranks = sb("ranks", [P, NQ, TB])
        slots = sb("slots", [P, NQ, TB])
        used = sb("used", [P, NQ])
        tokf = sb("tokf", [P, TB])
        tok = sb("tok", [P, 2, TB], I32)
        slot = sb("slot", [P, 2, TB], I32)
        nbefore = sb("nbefore", [P, P], F16)
        ones = sb("ones", [P, P], F16)
        tq = sb("tq", [P, 3, NQ])
        tcmp = sb("tcmp", [P, 2, NQ + 1])
        tone = sb("tone", [P, 2, NQ])
        tmul = sb("tmul", [P, 2, NQ])
        tval = sb("tval", [P, 3, 2])
        trow = sb("trow", [P, 2], I32)
        tokT = sb("tokT", [P, 2, P], I32)
        tokTf = sb("tokTf", [P, 2, P])
        tile_tok = sb("tile_tok", [P, 2 * P], I32)
        tile_exp = sb("tile_exp", [1, 2, 2 * P], I32)
        gidx = sb("gidx", [P, U], I32)
        sidx = sb("sidx", [P, U], I32)
        small = sb("small", [P, 256])
        inf2 = sb("inf2", [P, U, INFO_W])
        psum = ctx.enter_context(nc.psum_tensor("banks", [P, 8, 512], F32))

        tab = cst[:, 0:C * H].rearrange("p (c h) -> p c h", c=C)
        o = C * H
        ka, kw = cst[:, o:o + C], cst[:, o + C:o + 2 * C]
        o += 2 * C
        slope_c = cst[:, o:o + len(BLOCKS)]
        o += len(BLOCKS)
        ramp = cst[:, o:o + NE]
        o += NE
        key_c, first_c, second_c, region_c, row_c = (cst[:, o + NQ * i:o + NQ * (i + 1)] for i in range(5))
        o += 5 * NQ
        carry_c = cst[:, o:o + NQ * TB]
        o += NQ * TB
        tile_c = cst[:, o:o + 2]
        nbefore_c = cst[:, o + 2:o + 2 + P]

        raw = arena[:, 0:8192].rearrange("p (s c e) -> p s c e", s=LH, c=C)
        diff = arena[:, 0:NE * CH * E].rearrange("p (s c e) -> p s c e", s=NE, c=CH)
        prep = arena[:, 8192:8192 + C * E].rearrange("p (c e) -> p c e", c=C)
        quart = arena[:, 10240:10240 + 2 * CH * E].rearrange("p (s c e) -> p s c e", s=2, c=CH)
        scr = w_hi[:, :, :, :].rearrange("p s c e -> p (s c e)").bitcast(F32)
        x01 = scr[:, 0:1024]
        junk = scr[:, 1024:2048]
        tabf = scr[:, 2048:3072].rearrange("p (c h) -> p c h", c=C)
        cf = scr[:, 3072:4096].rearrange("p (s k h) -> p s k h", s=2, k=CH)
        welraw = scr[:, 4096:4096 + C * GOLAY_N].rearrange("p (c n) -> p c n", c=C)
        welpm = scr[:, 4224:4224 + C * GOLAY_N].rearrange("p (c n) -> p c n", c=C)
        msb = scr[:, 4352:4352 + C * GOLAY_N].rearrange("p (c n) -> p c n", c=C)
        rtr = scr[0:NE, 4608:4608 + E]
        wle = scr[0:96, 5120:5120 + E]
        wlpm = scr[0:96, 5632:5632 + E]
        wlh = scr[0:96, 6144:6144 + E // 2].bitcast(BF16)
        wlr = scr[0:96, 6656:6656 + E]
        wlm = scr[0:96, 7168:7168 + E // 2].bitcast(BF16)
        cqf = scr[:, 7680:7680 + H].rearrange("p (s q) -> p s q", s=2)
        xb = xbuf[:, :, :, :].rearrange("p u t e -> p (u t e)")
        lg = lat[:, 0:NE]
        eq, sc, oh1, oh2, l2, ex, dl, ux = (rsc[:, i] for i in range(8))
        (m1, m2, mx1, mx2, zs, d2, e2, p1, p2, den, w1, w2, u1, u2, nlow, nhigh, fix, kmax, kmin, isa, isb,
         wa1, wa2, wb1, wb2, slotf) = (rsm[:, i] for i in range(26))
        oh12, ux12 = rsc[:, 2:4], rsc[:, 6:8]
        p12, w12, u12, isab, wa12 = (rsm[:, i:i + 2] for i in (7, 10, 12, 19, 21))
        far = xT4[:, :, :, :].rearrange("p b c n -> p (b c n)").bitcast(I32)[:, 0:TROWS]
        info_bits = info[:, :, 16:64].bitcast(BF16).rearrange("p t (g c) -> p t g c", g=3)

        def two(t, i):
            return t[:, i:i + 2 * E].rearrange("p (s e) -> p s e", s=2)

        def two16(t, i):
            return t[:, i:i + E].bitcast(F16).rearrange("p (s e) -> p s e", s=2)
        x2 = xb[:, 0:U * E].rearrange("p (s e) -> p s e", s=U)
        raw2, uv2, o2, ysb2, s2, sg2 = (two(xb, U * E + 2 * E * i) for i in range(6))
        yp2 = raw2[:, :, H:E]
        t2, z2, g2 = (two(arena, 2 * E * i) for i in range(3))
        hi2, lo2 = (two16(arena, 6 * E + E * i) for i in range(2))
        hl2 = arena[:, 8 * E:10 * E].bitcast(F16).rearrange("p (s v c e) -> p s v c e", s=2, v=2, c=C)
        bT2 = arena[0:96, 10 * E:10 * E + P].bitcast(BF16).rearrange("p (s e) -> p s e", s=2)

        v, at = {}, 0
        for name, m in (("st", 12), ("mv", 4), ("ve", 2), ("sd", 2), ("r0", 2), ("rt", 2), ("mu", 5), ("cnt", 5), ("ly", 5),
                        ("D", 1), ("wD", 1), ("a", 1), ("b", 1), ("arg", C), ("ph", C), ("s1", C), ("q1", C), ("q2", C)):
            v[name] = small[:, at:at + m]
            at += m
        v["st"] = v["st"].rearrange("p (r k) -> p r k", r=2)
        v["mv"] = v["mv"].rearrange("p (r k) -> p r k", r=2)

        def sems(names):
            return [sem(x) for x in names.split()]
        ld_x01, ld_cst, ld_small, ld_router = sems("ld_x01 ld_cst ld_small ld_router")
        ld_w = [sem(f"ld_w{i}") for i in range(LH)]
        ld_prep = sem("ld_prep")
        ld_x = [sem(f"ld_x{i}") for i in range(U)]
        dch, pch, d_ready, act_setup, filt_ready = sems("vector_chain pool_chain d_ready act_setup filt_ready")
        ident_ready, ones_ready, info_init, zeroed, far_ready, far_stored = sems(
            "ident_ready ones_ready info_init zeroed far_ready far_stored")
        c_mm, c_copied, c_lo_ready, m_mm, wel_ready, m_copied, rt_mm, wcat_raw, wmean_mm, wcat_ready, wle_ready = sems(
            "c_mm c_copied c_lo_ready m_mm wel_ready m_copied rt_mm wcat_raw wmean_mm wcat_ready wle_ready")
        norm_ready, norm_red, norm_root, wsc_ready, wpm_ready, whi_ready, wsum_ready, wlo_ready = sems(
            "norm_ready norm_red norm_root wsc_ready wpm_ready whi_ready wsum_ready wlo_ready")
        sort_init, iota_ready = sems("sort_init iota_ready")
        t1_done, t1_copied, mm1_done, latT_copied, back_done, lat_copied = sems(
            "t1_done t1_copied mm1_done latT_copied back_done lat_copied")
        stats_ready, aggr_ready, var_ready, sd_ready, newton, rstd_ready = sems(
            "stats_ready aggr_ready var_ready sd_ready newton rstd_ready")
        route_a, route_c, route_d, dx_ready, exp_ready, corr_ready, bits_copied = sems(
            "route_a route_c route_d dx_ready exp_ready corr_ready bits_copied")
        pairs_ready, rank_mm, slot_ready, scattered, info_ready, info_stored = sems(
            "pairs_ready rank_mm slot_ready scattered info_ready info_stored")
        slot_seen, latT_seen, o_seen = sems("slot_seen latT_seen o_seen")
        prep_seen = sem("prep_seen")
        wdiff_ready, wadd_ready = sems("wdiff_ready wadd_ready")
        rows_ready, rows_loaded, rows_float, rows_turned, exps_mm, tiles_ready = sems(
            "rows_ready rows_loaded rows_float rows_turned exps_mm tiles_ready")
        ld_x2 = [sem(f"ld_x2_{i}") for i in range(U)]
        stored = [sem(f"stored{i}") for i in range(2)]
        inf_init, gidx_ready, sidx_ready, raw_ready, uv_ready, hi_ready, split_ready = sems(
            "inf_init gidx_ready sidx_ready raw_ready uv_ready hi_ready split_ready")
        uvT_done, hl_ready, e_done, t_ready, z_ready, g_ready, y_done, y_copied, s_ready, sg_ready, o_ready = sems(
            "uvT_done hl_ready e_done t_ready z_ready g_ready y_done y_copied s_ready sg_ready o_ready")
        yp_ready = sem("yp_ready")

        TURN = (0, 1, 3, 5)

        block = ctx.enter_context(nc.Block())

        def after(eng, s, v):
            if isinstance(v, int) and v <= 0:
                return
            eng.wait_ge(s, v)

        def rounds(eng, count, step, head=1):
            for i in range(head):
                for k in range(U):
                    step(i, k)
            with eng.Fori(head, count - 1) as i:
                for k in range(U):
                    step(i, k)
            for k in range(U):
                step(count - 1, k, last=True)

        def at(i, k, ahead):
            return i + (k + ahead) // U, (k + ahead) % U

        def later_than_first(i):
            return not (isinstance(i, int) and i == 0)

        @block.sync
        def _(sp):
            sp.dma_start(x01, x_rows[0:2, :].rearrange("n e -> (n e)").partition_broadcast(P)).then_inc(ld_x01, 16)
            sp.dma_start(cst[:, :], consts).then_inc(ld_cst, 16)
            sp.dma_start(welraw, W_el.rearrange("(c p) n -> p c n", p=P)).then_inc(ld_small, 16)
            sp.dma_start(bel[:, :], b_el.partition_broadcast(P)).then_inc(ld_small, 16)
            sp.wait_ge(zeroed, 1)
            for g in range(3):
                sp.dma_start(wle[32 * g:32 * g + GOLAY_N, :], W_le).then_inc(ld_small, 16)
                sp.dma_start(wle[32 * g + GOLAY_N:32 * g + GOLAY_N + 1, :], b_le.rearrange("(a e) -> a e", a=1)).then_inc(ld_small, 16)
            sp.dma_start(rtr, router_w).then_inc(ld_router, 16)
            def load(i, k):
                after(sp, t1_done, GT * ((i - 1) * U + k + 1))
                after(sp, stats_ready, (i - 1) * U + k + 1)
                sp.dma_start(xbuf[:, k], x_tiles[:, bass.ds((i * U + k) * GT, GT), :]).then_inc(ld_x[k], 16)

            def load_for_norm(e):
                after(sp, norm_ready, e - LH + 1)
                sp.dma_start(raw[:, e % LH], experts[e].rearrange("(c p) o -> p c o", p=P)).then_inc(ld_w[e % LH], 16)

            def load_expert(e):
                after(sp, wpm_ready, e)
                sp.dma_start(prep, expert_rows[:, bass.ds(e, 1)].rearrange("p o c n -> p (o c) n")).then_inc(ld_prep, 16)
            load_for_norm(0)
            load_for_norm(1)
            load(0, 0)
            sp.wait_ge(far_ready, 1)
            sp.dma_start(pair_tokens.rearrange("(p r) c -> p (r c)", p=P), far).then_inc(far_stored, 16)
            load(0, 1)
            for e in range(2, NE):
                load_for_norm(e)
                if e < U:
                    load(0, e)
            load_expert(0)
            for k in range(U):
                load(1, k)
            load_expert(1)
            with sp.Fori(2, R) as i:
                for k in range(U):
                    load(i, k)
                load_expert(i)

        @block.gpsimd
        def _(pool):
            G = nc.gpsimd
            n = [0]

            def link(ins):
                n[0] += 1
                ins.then_inc(pch, 1)
                pool.wait_ge(pch, n[0])
            G.memset(wle, 0.0).then_inc(zeroed, 1)
            G.memset(wcat[:, :, :], 0.0).then_inc(zeroed, 1)
            G.memset(avg[:, :], 1.0 / E)
            G.memset(ones[:, :], 1.0).then_inc(ones_ready, 1)
            link(G.memset(ident[:, :], 0.0))
            G.affine_select(out=ident[:, :], in_=ident[:, :], compare_op=ALU.not_equal, fill=1.0, base=0,
                            pattern=[[-1, P]], channel_multiplier=1).then_inc(ident_ready, 1)
            pool.wait_ge(ident_ready, 1)
            G.tensor_copy(ident_b[:, :], ident[:, :])
            G.tensor_copy(ident_h[:, :], ident[:, :]).then_inc(ident_ready, 1)
            G.memset(far, FAR).then_inc(far_ready, 1)
            G.iota(tok[:, 1, :], pattern=[[P, TB]], base=-P * TB, channel_multiplier=1).then_inc(iota_ready, 1)
            link(G.memset(info[:, :, :], 0.0))
            G.memset(info_bits[:, :, :, GOLAY_N:GOLAY_N + 1], 1.0).then_inc(info_init, 1)
            pool.wait_ge(norm_ready, NE)
            G.partition_all_reduce(norm_all[:, :], norm2[:, :], P, RMAX).then_inc(norm_red, 1)

            def halves(e, buf=0):
                h2 = quart[:, buf]
                if not isinstance(e, int):
                    pool.wait_ge(wsum_ready, e)
                pool.wait_ge(ld_prep, 16 * (e + 1))
                pool.sem_inc(prep_seen, 1)
                G.tensor_tensor(diff[:, bass.ds(e, 1)].rearrange("p o c n -> p (o c) n"), prep[:, 0:CH], prep[:, CH:C],
                                ALU.subtract).then_inc(wdiff_ready, 1)
                pool.wait_ge(wdiff_ready, e + 1)
                G.tensor_tensor(prep[:, 0:CH], prep[:, 0:CH], prep[:, CH:C], ALU.add).then_inc(wadd_ready, 1)
                pool.wait_ge(wadd_ready, e + 1)
                G.tensor_tensor(h2[:, 0], prep[:, 0], prep[:, 1], ALU.add)
                G.tensor_tensor(h2[:, 1], prep[:, 0], prep[:, 1], ALU.subtract).then_inc(wpm_ready, 1)
            def scatter(i, buf=0):
                pool.wait_ge(slot_ready, i + 1)
                pool.sem_inc(slot_seen, 1)
                for t in range(TB):
                    pool.indirect_dma_start(
                        out=pair_slots, out_offset=bass.IndirectOffsetOnAxis(ap=slot[:, buf, t:t + 1], axis=0),
                        in_=tok[:, buf, t:t + 1], in_offset=None).then_inc(scattered, 16)
            halves(0)
            halves(1, 1)
            pool.wait_ge(far_stored, 16)
            with pool.Fori(0, R - 2) as i:
                scatter(i)
                halves(i + 2)
            scatter(R - 2)
            scatter(R - 1, 1)
            pool.wait_ge(scattered, 16 * T)
            pool.wait_ge(rows_ready, 1)
            for h in range(2):
                pool.indirect_dma_start(out=tokT[:, h], out_offset=None, in_=pair_tokens,
                                        in_offset=bass.IndirectOffsetOnAxis(ap=trow[:, h:h + 1], axis=0)).then_inc(rows_loaded, 16)
            G.memset(inf2[:, :, :], 0.0).then_inc(inf_init, 1)
            pool.wait_ge(inf_init, 1)
            pool.wait_ge(info_stored, 16 * R)

            def gather(k):
                tokens = bass.IndirectOffsetOnAxis(ap=gidx[:, k:k + 1], axis=0)
                pool.indirect_dma_start(out=x2[:, k], out_offset=None, in_=x_rows, in_offset=tokens,
                                        bounds_check=N - 1, oob_is_err=False).then_inc(ld_x2[k], 16)
                pool.indirect_dma_start(out=inf2[:, k], out_offset=None, in_=info_dram, in_offset=tokens,
                                        bounds_check=N - 1, oob_is_err=False).then_inc(ld_x2[k], 16)

            def scatter_out(k):
                pool.indirect_dma_start(out=out_rows, out_offset=bass.IndirectOffsetOnAxis(ap=sidx[:, k:k + 1], axis=0),
                                        in_=o2[:, k % 2], in_offset=None,
                                        bounds_check=N - 1, oob_is_err=False).then_inc(stored[k % 2], 16)

            def step(i, k, last=False):
                j, b = i * U + k, k % 2
                pool.wait_ge(sg_ready, j + 1)
                after(pool, stored[b], 16 * (i * (U // 2) + k // 2))
                G.tensor_tensor(o2[:, b], sg2[:, b], x2[:, k], ALU.add).then_inc(o_ready, 1)
                pool.wait_ge(sidx_ready, j + 1)
                if not last:
                    pool.wait_ge(gidx_ready, j + U + 1)
                pool.wait_ge(o_ready, j + 1)
                pool.sem_inc(o_seen, 1)
                if not last:
                    gather(k)
                scatter_out(k)
            for k in range(U):
                pool.wait_ge(gidx_ready, k + 1)
                gather(k)
            rounds(pool, NT // U, step)
            for b in range(2):
                pool.wait_ge(stored[b], 16 * (NT // 2))

        @block.scalar
        def _(act):
            def norm(e):
                act.wait_ge(ld_w[e % LH], 16 * (e // LH + 1))
                nc.scalar.activation(w_lo[:, e].bitcast(BF16), raw[:, e % LH], ACT.Square,
                                     accum_out=norm2[:, e:e + 1]).then_inc(norm_ready, 1)
            act.wait_ge(d_ready, 1)
            nc.scalar.activation(v["sd"], v["ve"], ACT.Sqrt).then_inc(act_setup, 1)
            act.wait_ge(d_ready, 2)
            nc.scalar.activation(v["ly"], v["cnt"], ACT.Ln).then_inc(act_setup, 1)
            act.wait_ge(d_ready, 3)
            nc.scalar.activation(v["s1"], v["arg"], ACT.Sin, scale=0.5)
            nc.scalar.activation(v["q1"], v["arg"], ACT.Sin, scale=0.25)
            nc.scalar.activation(v["q2"], v["ph"], ACT.Sin, scale=0.5).then_inc(act_setup, 1)
            norm(0)
            norm(1)
            for s in range(2):
                act.wait_ge(c_mm, s + 1)
                cps = psum[:, s].rearrange("p (k h) -> p k h", k=CH)
                last = nc.scalar.activation(cf[:, s], cps, ACT.Copy)
                if s == 1:
                    last = nc.scalar.activation(c_hi[:, :, :], cps, ACT.Copy)
                last.then_inc(c_copied, 1)
            act.wait_ge(m_mm, 1)
            nc.scalar.activation(msb, psum[:, 2, 0:C * GOLAY_N].rearrange("p (c n) -> p c n", c=C), ACT.Copy,
                                 scale=1.0 / CS).then_inc(m_copied, 1)
            act.wait_ge(rt_mm, 1)
            nc.scalar.activation(wcat[:, :, 0:NE], psum[:, 3, 0:C * NE].rearrange("p (c n) -> p c n", c=C),
                                 ACT.Copy).then_inc(m_copied, 1)
            norm(2)
            norm(3)

            def high(e, scale, buf=0):
                parts = w_hi[:, bass.ds(e, 1)].rearrange("p o c n -> p (o c) n")
                nc.scalar.activation(parts[:, 0:CH], quart[:, buf], ACT.Copy, scale=scale[:, 1:2])
                nc.scalar.activation(parts[:, CH:C], diff[:, bass.ds(e, 1)].rearrange("p o c n -> p (o c) n"), ACT.Copy,
                                     scale=scale[:, 0:1]).then_inc(whi_ready, 1)

            def turn_copy(i, k, q):
                t = (i * U + k) * GT + q
                act.wait_ge(t1_done, t + 1)
                if q == 0:
                    after(act, mm1_done, i * U + k - 1)
                nc.scalar.activation(xT4[:, k % 2, :, q * P:(q + 1) * P], psum[:, TURN[q]].rearrange("p (c n) -> p c n", c=C),
                                     ACT.Copy).then_inc(t1_copied, 1)

            def latT_copy(i, k):
                g = i * U + k
                act.wait_ge(mm1_done, g + 1)
                after(act, back_done, g - 1)
                nc.scalar.activation(latT[:, k % 2], psum[:, 2], ACT.Copy).then_inc(latT_copied, 1)

            def exps(n):
                act.wait_ge(dx_ready, n + 1)
                nc.scalar.activation(ex, dl, ACT.Exp)
                nc.scalar.activation(e2, d2, ACT.Exp).then_inc(exp_ready, 1)

            def bits_copy(n):
                act.wait_ge(corr_ready, n + 1)
                after(act, info_stored, 16 * n)
                for c in range(3):
                    last = nc.scalar.activation(info_bits[:, :, c, 0:GOLAY_N], bits.rearrange("p n t -> p t n"), ACT.Copy)
                last.then_inc(bits_copied, 1)

            def info_store(n):
                act.wait_ge(info_ready, n + 1)
                act.wait_ge(bits_copied, n + 1)
                act.dma_start(info_tiles[:, bass.ds(n * TB, TB), :], info[:, :, :]).then_inc(info_stored, 16)

            def step1(i, k, last=False):
                ahead = not (last and k + 1 >= U)
                later = later_than_first(i)
                second = isinstance(i, int) and i == 1
                if ahead:
                    turn_copy(*at(i, k, 1), 0)
                    turn_copy(*at(i, k, 1), 1)
                if later and k == 3:
                    act.wait_ge(wpm_ready, i + 1)
                    act.wait_ge(wsc_ready, i)
                latT_copy(i, k)
                if ahead:
                    turn_copy(*at(i, k, 1), 2)
                    turn_copy(*at(i, k, 1), 3)
                if not later:
                    norm(LH + k)
                if second and k == 0:
                    act.wait_ge(norm_red, 1)
                    nc.scalar.activation(norm_all[:, :], norm_all[:, :], ACT.Sqrt).then_inc(norm_root, 1)
                if later and k == 1:
                    exps(i - 1)
                    bits_copy(i - 1)
                if k == 2:
                    act.wait_ge(var_ready, i + 1)
                    nc.scalar.activation(rt1[:, 1], rt1[:, 0], ACT.Sqrt).then_inc(sd_ready, 1)
                if later and not second and k == 0:
                    info_store(i - 2)
                if later and k == 3:
                    if second:
                        high(0, wscale[:, 0])
                        high(1, wscale[:, 1], 1)
                    else:
                        high(i, wsc[:, 0])
            act.wait_ge(far_stored, 16)
            act.wait_ge(info_init, 1)
            for q in range(GT):
                turn_copy(0, 0, q)
            rounds(act, R, step1, head=2)
            info_store(R - 2)
            exps(R - 1)
            bits_copy(R - 1)
            info_store(R - 1)
            def front(i, k):
                j, b = i * U + k, k % 2
                act.wait_ge(uvT_done, j + 1)
                after(act, y_done, j - 1)
                nc.scalar.activation(hl2[:, b], psum[:, 0].bitcast(F16).rearrange("p (v c n) -> p v c n", v=2, c=C), ACT.Copy)
                nc.scalar.activation(bT2[:, b], psum[0:96, 1, 0:P // 2].bitcast(BF16), ACT.Copy).then_inc(hl_ready, 1)

            def step(i, k, last=False):
                j, b = i * U + k, k % 2
                act.wait_ge(e_done, 2 * j + 1)
                after(act, z_ready, j - 1)
                nc.scalar.activation(t2[:, b], psum[:, 4 + b], ACT.Identity, scale=inf2[:, k, 3:4],
                                     bias=inf2[:, k, 2:3]).then_inc(t_ready, 1)
                if not (last and k + 1 >= U):
                    front(*at(i, k, 1))
                act.wait_ge(z_ready, j + 1)
                after(act, sg_ready, j - 1)
                nc.scalar.activation(g2[:, b], z2[:, b], ACT.Silu).then_inc(g_ready, 1)
                act.wait_ge(y_done, j + 1)
                after(act, s_ready, j - 1)
                nc.scalar.activation(ysb2[:, b, Q:E], psum[:, 2 + b, Q:E], ACT.Copy, scale=1.0 / (XS * CS)).then_inc(y_copied, 1)
            front(0, 0)
            rounds(act, NT // U, step)

        @block.vector
        def _(dve):
            n = [0]

            def link(ins):
                n[0] += 1
                ins.then_inc(dch, 1)
                dve.wait_ge(dch, n[0])

            def chain(s, base):
                c = [0]

                def link_in(ins, beside=None):
                    c[0] += 1
                    ins.then_inc(s, 1)
                    if beside:
                        beside()
                    dve.wait_ge(s, base + c[0])
                return link_in
            V = nc.vector
            dve.wait_ge(ld_x01, 16)
            for r in range(2):
                last = V.bn_stats(v["st"][:, r], x01[:, r * E:(r + 1) * E])
            link(last)
            for r in range(2):
                last = V.bn_aggr(v["mv"][:, r], v["st"][:, r])
            link(last)
            V.tensor_scalar(v["ve"], v["mv"][:, :, 1], EPS, None, ALU.add).then_inc(d_ready, 1)
            dve.wait_ge(act_setup, 1)
            link(V.reciprocal(v["r0"], v["sd"]))
            link(V.tensor_tensor(v["rt"], v["r0"], v["r0"], ALU.mult))
            link(V.tensor_tensor(v["rt"], v["rt"], v["ve"], ALU.mult))
            link(V.tensor_scalar(v["rt"], v["rt"], -0.5, 1.5, ALU.mult, ALU.add))
            link(V.tensor_tensor(v["r0"], v["r0"], v["rt"], ALU.mult))
            for r in range(2):
                last = V.tensor_scalar(junk[:, r * E:(r + 1) * E], x01[:, r * E:(r + 1) * E], v["mv"][:, r, 0:1],
                                       v["r0"][:, r:r + 1], ALU.subtract, ALU.mult)
            link(last)
            for c, side in enumerate(BLOCKS):
                last = V.tensor_reduce(v["mu"][:, c:c + 1], junk[:, 0:side * side], AXX, ALU.add)
            link(last)
            for c, side in enumerate(BLOCKS):
                last = V.tensor_scalar(v["mu"][:, c:c + 1], v["mu"][:, c:c + 1], 1.0 / (side * side), None, ALU.mult)
            link(last)
            for c, side in enumerate(BLOCKS):
                link(V.tensor_scalar(x01[:, 0:side * side], junk[:, 0:side * side], v["mu"][:, c:c + 1], 0.0, ALU.is_gt,
                                     ALU.add, accum_out=v["cnt"][:, c:c + 1]))
            V.tensor_scalar(v["cnt"], v["cnt"], 1.0, None, ALU.max).then_inc(d_ready, 1)
            dve.wait_ge(ld_cst, 16)
            dve.wait_ge(act_setup, 2)
            link(V.tensor_tensor(v["ly"], v["ly"], slope_c, ALU.mult))
            link(V.tensor_reduce(v["D"], v["ly"], AXX, ALU.add))
            link(V.tensor_scalar(v["D"], v["D"], 1.0, 2.0, ALU.max, ALU.min))
            V.tensor_scalar(v["wD"], v["D"], 0.2, 1.0, ALU.mult, ALU.add)
            V.tensor_scalar(v["a"], v["D"], 0.5, 1.0, ALU.mult, ALU.add)
            V.tensor_scalar(v["b"], v["D"], 0.1, None, ALU.mult)
            link(V.tensor_tensor(v["ph"], ka, ka, ALU.mult))
            link(V.tensor_tensor(v["wD"], v["wD"], v["D"], ALU.mult))
            V.tensor_scalar(v["arg"], ka, v["a"], v["wD"], ALU.mult, ALU.add)
            link(V.scalar_tensor_tensor(v["ph"], v["ph"], v["b"], ka, ALU.mult, ALU.subtract))
            V.tensor_scalar(v["ph"], v["ph"], v["wD"], None, ALU.add).then_inc(d_ready, 1)
            dve.wait_ge(act_setup, 3)
            V.tensor_tensor(v["q1"], v["q1"], v["q1"], ALU.mult)
            link(V.tensor_tensor(v["q2"], v["q2"], v["q2"], ALU.mult))
            V.tensor_scalar(v["q1"], v["q1"], -2.0, 1.0, ALU.mult, ALU.add)
            link(V.tensor_scalar(v["q2"], v["q2"], -2.0, 1.0, ALU.mult, ALU.add))
            link(V.tensor_tensor(v["q1"], v["q1"], v["q2"], ALU.mult))
            link(V.tensor_tensor(v["q1"], v["q1"], v["s1"], ALU.mult))
            link(V.tensor_tensor(v["q1"], v["q1"], kw, ALU.mult))
            for c in range(C):
                last = V.tensor_scalar(tabf[:, c], tab[:, c], v["q1"][:, c:c + 1], 2.0 * CS, ALU.mult, ALU.mult)
            last.then_inc(filt_ready, 1)
            dve.wait_ge(ld_small, 16 * 8)
            V.tensor_tensor(welpm[:, 0:CH], welraw[:, 0:CH], welraw[:, CH:C], ALU.add)
            V.tensor_tensor(welpm[:, CH:C], welraw[:, 0:CH], welraw[:, CH:C], ALU.subtract).then_inc(wel_ready, 1)
            V.tensor_scalar(bel[:, :], bel[:, :], -1.0, None, ALU.mult)
            V.tensor_tensor(wlr[:, 0:H], wle[:, 0:H], wle[:, H:E], ALU.add)
            link(V.tensor_tensor(wlpm[:, H:E], wle[:, 0:H], wle[:, H:E], ALU.subtract))
            V.tensor_tensor(wlpm[:, 0:Q], wlr[:, 0:Q], wlr[:, Q:H], ALU.add)
            link(V.tensor_tensor(wlpm[:, Q:H], wlr[:, 0:Q], wlr[:, Q:H], ALU.subtract))
            link(V.tensor_scalar(wlpm[:, 0:H], wlpm[:, 0:H], 0.5, None, ALU.mult))
            half = XS * CS / 2
            link(V.tensor_scalar(wlh, wlpm, half, None, ALU.mult))
            link(V.scalar_tensor_tensor(wlr, wlpm, half, wlh, ALU.mult, ALU.subtract))
            link(V.tensor_copy(wlm, wlr))
            V.tensor_copy(wle3[0:32], wlh[0:32])
            V.tensor_copy(wle3[32:64], wlm[32:64])
            V.tensor_tensor(wle3[64:96], wlr[64:96], wlm[64:96], ALU.subtract).then_inc(wle_ready, 1)
            dve.wait_ge(c_copied, 1)
            V.tensor_tensor(cqf[:, 0], cf[:, 0, 0, 0:Q], cf[:, 0, 0, Q:H], ALU.add)
            link(V.tensor_tensor(cqf[:, 1], cf[:, 0, 0, 0:Q], cf[:, 0, 0, Q:H], ALU.subtract))
            link(V.tensor_scalar(cq_hi[:, :, :], cqf, 0.5, None, ALU.mult))
            V.scalar_tensor_tensor(cq_lo[:, :, :], cqf, 0.5, cq_hi[:, :, :], ALU.mult, ALU.subtract).then_inc(c_lo_ready, 1)
            dve.wait_ge(c_copied, 2)
            V.tensor_tensor(c_lo[:, :, :], psum[:, 1].rearrange("p (k h) -> p k h", k=CH), c_hi[:, :, :],
                            ALU.subtract).then_inc(c_lo_ready, 1)
            V.tensor_copy(nbefore[:, :], nbefore_c)
            V.tensor_copy(used[:, :], region_c).then_inc(sort_init, 1)
            dve.wait_ge(iota_ready, 1)
            link(V.tensor_copy(tokf[:, :], tok[:, 1, :]))
            dve.wait_ge(m_copied, 2)
            dve.wait_ge(zeroed, 2)
            V.tensor_tensor(wcat[:, 0:CH, NE:NL], msb[:, 0:CH], msb[:, CH:C], ALU.add)
            V.tensor_tensor(wcat[:, CH:C, NE:NL], msb[:, 0:CH], msb[:, CH:C], ALU.subtract).then_inc(wcat_raw, 1)
            dve.wait_ge(wmean_mm, 1)
            V.tensor_tensor(wcat[:, :, 0:NL], wcat[:, :, 0:NL], psum[:, 4, 0:NL].unsqueeze(1).broadcast_to([P, C, NL]),
                            ALU.subtract).then_inc(wcat_ready, 1)

            def scales():
                dve.wait_ge(norm_root, 1)
                link(V.tensor_scalar(norm_all[:, :], norm_all[:, :], 1e-18, None, ALU.max))
                link(V.reciprocal(wscale[:, :, 0], norm_all[:, :]))
                V.tensor_scalar(unscale[:, :], norm_all[:, :], 0.5 / (XS * WS), None, ALU.mult)
                V.tensor_scalar(wscale[:, :, 1], wscale[:, :, 0], WS / 2, None, ALU.mult)
                link(V.tensor_scalar(wscale[:, :, 0], wscale[:, :, 0], WS, None, ALU.mult))
                dve.sem_inc(wsc_ready, 1)

            def scale_of(e):
                V.tensor_copy(wsc[:, :, :], wscale[:, bass.ds(e, 1), :]).then_inc(wsc_ready, 1)

            def low_sums(e, scale, buf=0):
                lo, hi = (t[:, bass.ds(e, 1), 0:CH].rearrange("p o c n -> p (o c) n") for t in (w_lo, w_hi))
                dve.wait_ge(whi_ready, e + 1)
                V.scalar_tensor_tensor(lo, quart[:, buf], scale[:, 1:2], hi, ALU.mult, ALU.subtract).then_inc(wsum_ready, 1)

            def low_differences(e):
                V.scalar_tensor_tensor(w_lo[:, e, CH:C], diff[:, e], wscale[:, e, 0:1], w_hi[:, e, CH:C], ALU.mult,
                                       ALU.subtract).then_inc(wlo_ready, 1)

            def stat(i, k, q):
                if q == 0:
                    dve.wait_ge(ld_x[k], 16 * (i + 1))
                ins = V.bn_stats(st6[:, k * GT + q], xbuf[:, k, q])
                if q == GT - 1:
                    ins.then_inc(stats_ready, 1)

            def deviations(i):
                dve.wait_ge(stats_ready, U * (i + 1))
                V.tensor_copy(rt1[:, 3], st6[:, :, 0])
                for t in range(TB):
                    last = V.bn_aggr(mv1[:, t], st6[:, t])
                last.then_inc(aggr_ready, 1)
                dve.wait_ge(aggr_ready, i + 1)
                V.tensor_scalar(rt1[:, 0], mv1[:, :, 1], EPS, None, ALU.add).then_inc(var_ready, 1)

            NONE = [None] * (U - 1) * GT

            def newton_steps(i):
                ve, sd, r0, rt = (rt1[:, c] for c in range(4))

                def first():
                    dve.wait_ge(sd_ready, i + 1)
                    V.reciprocal(r0, sd).then_inc(newton, 1)

                def square():
                    dve.wait_ge(newton, 4 * i + 1)
                    V.tensor_tensor(rt, r0, r0, ALU.mult).then_inc(newton, 1)

                def product():
                    dve.wait_ge(newton, 4 * i + 2)
                    V.tensor_tensor(rt, rt, ve, ALU.mult).then_inc(newton, 1)

                def factor():
                    dve.wait_ge(newton, 4 * i + 3)
                    V.tensor_scalar(rt, rt, -0.5, 1.5, ALU.mult, ALU.add).then_inc(newton, 1)

                def final():
                    dve.wait_ge(newton, 4 * i + 4)
                    V.tensor_scalar(mean4[:, :], mv1[:, :, 0], 4.0, None, ALU.mult)
                    V.tensor_tensor(rstd[:, :], r0, rt, ALU.mult).then_inc(rstd_ready, 1)
                return [first, square, product, factor, final]

            def over(a):
                return a.rearrange("p n t -> p t n")

            def each(a, m):
                return a.unsqueeze(1).broadcast_to([P, m, TB])

            def along(a, m):
                return a.unsqueeze(2).broadcast_to([P, m, TB])


            def tiles_of(i, k):
                return [lambda q=q: stat(i, k, q) for q in range(GT)]

            def choose(n, beside=NONE):
                lk = chain(route_a, 12 * n)
                dve.wait_ge(rstd_ready, n + 1)
                dve.wait_ge(back_done, U * (n + 1))
                V.tensor_tensor(lat[:, :, :], psum[:, 4, 0:TB * NL].rearrange("p (t n) -> p n t", n=NL), each(rstd[:, :], NL),
                                ALU.mult).then_inc(lat_copied, 1)
                dve.wait_ge(lat_copied, n + 1)
                after(dve, bits_copied, n)
                V.tensor_tensor(bits[:, :, :], lat[:, NE:NL], along(bel[:, :], GOLAY_N), ALU.is_gt)
                lk(V.tensor_reduce(m1, over(lg), AXX, ALU.max), beside[0])
                V.tensor_reduce(nlow, over(bits[:, 0:GOLAY_R]), AXX, ALU.add)
                V.tensor_reduce(nhigh, over(bits[:, GOLAY_R:]), AXX, ALU.add)
                lk(V.tensor_tensor(eq, lg, each(m1, NE), ALU.is_equal), beside[1])
                V.scalar_tensor_tensor(fix, nlow, 4.0, nhigh, ALU.mult, ALU.add)
                lk(V.tensor_tensor(sc, eq, along(ramp, NE), ALU.mult), beside[2])
                V.tensor_scalar(fix, fix, 3.0, None, ALU.is_le)
                lk(V.tensor_reduce(mx1, over(sc), AXX, ALU.max), beside[3])
                V.tensor_tensor(fixadd[:, :, :], bits[:, GOLAY_R:], each(fix, GOLAY_R), ALU.mult)
                lk(V.tensor_tensor(oh1, sc, each(mx1, NE), ALU.is_equal), beside[4])
                V.tensor_tensor(bits[:, 0:GOLAY_R], bits[:, 0:GOLAY_R], fixadd[:, :, :], ALU.add).then_inc(corr_ready, 1)
                lk(V.scalar_tensor_tensor(l2, oh1, -3e38, lg, ALU.mult, ALU.add), beside[5])
                V.tensor_tensor(dl, lg, each(m1, NE), ALU.subtract)
                lk(V.tensor_reduce(m2, over(l2), AXX, ALU.max), beside[6])
                V.tensor_tensor(d2, m2, m1, ALU.subtract).then_inc(dx_ready, 1)
                lk(V.tensor_tensor(eq, l2, each(m2, NE), ALU.is_equal), beside[7])
                lk(V.tensor_tensor(sc, eq, along(ramp, NE), ALU.mult), beside[8])
                lk(V.tensor_reduce(mx2, over(sc), AXX, ALU.max), beside[9])
                V.tensor_tensor(oh2, sc, each(mx2, NE), ALU.is_equal)
                V.tensor_tensor(kmin, mx1, mx2, ALU.min)
                V.tensor_tensor(isa, mx1, mx2, ALU.is_gt)
                lk(V.tensor_tensor(kmax, mx1, mx2, ALU.max), beside[10])
                V.tensor_scalar(isb, isa, -1.0, 1.0, ALU.mult, ALU.add)
                lk(V.scalar_tensor_tensor(kmax, kmax, float(NE), kmin, ALU.mult, ALU.add), beside[11])
                V.tensor_tensor(pairs[:, :, :], each(kmax, NQ), along(key_c, NQ), ALU.is_equal).then_inc(pairs_ready, 1)

            def weigh(n, beside=NONE):
                lk = chain(route_c, 9 * n)
                dve.wait_ge(exp_ready, n + 1)
                V.tensor_reduce(zs, over(ex), AXX, ALU.add)
                after(dve, info_stored, 16 * n)
                V.tensor_copy(info[:, :, 0], mean4[:, :])
                V.tensor_scalar(info[:, :, 1], rstd[:, :], XS, None, ALU.mult)
                lk(V.tensor_tensor(ux12, oh12, unscale[:, :].unsqueeze(1).unsqueeze(3).broadcast_to([P, 2, NE, TB]), ALU.mult),
                   beside[0])
                V.tensor_reduce(u12, ux12.rearrange("p s n t -> p s t n"), AXX, ALU.add)
                lk(V.reciprocal(p1, zs), beside[1])
                lk(V.tensor_tensor(p2, e2, p1, ALU.mult), beside[2])
                lk(V.tensor_tensor(den, p1, p2, ALU.add), beside[3])
                lk(V.tensor_scalar(den, den, 1e-6, None, ALU.add), beside[4])
                lk(V.reciprocal(den, den))
                lk(V.tensor_tensor(w12, p12, each(den, 2), ALU.mult))
                V.tensor_tensor(p12, p12, w12, ALU.mult)
                lk(V.tensor_tensor(u12, u12, w12, ALU.mult))
                V.tensor_tensor(info[:, :, 2], p1, p2, ALU.add)
                V.tensor_tensor(wb1, isb, u1, ALU.mult)
                V.tensor_tensor(wb2, isa, u2, ALU.mult)
                lk(V.tensor_tensor(wa12, isab, u12, ALU.mult))
                V.tensor_tensor(info[:, :, 3], wa12[:, 0], wa12[:, 1], ALU.add)
                V.tensor_tensor(info[:, :, 4], wb1, wb2, ALU.add).then_inc(info_ready, 1)

            def place(n, buf=0, beside=NONE):
                lk = chain(route_d, 5 * n)
                totals = psum[:, 7, 0:NQ * TB].rearrange("p (q t) -> p q t", q=NQ)
                within = psum[:, 6, 0:NQ * TB].rearrange("p (q t) -> p q t", q=NQ)
                dve.wait_ge(rank_mm, n + 1)
                V.tensor_scalar(tokf[:, :], tokf[:, :], float(P * TB), None, ALU.add)
                lk(V.tensor_tensor(totals[:, :, 0], totals[:, :, 0], used[:, :], ALU.add), beside[0])
                lk(V.tensor_tensor_scan(ranks.rearrange("p q t -> p (q t)"), carry_c, psum[:, 7, 0:NQ * TB], 0.0,
                                        ALU.mult, ALU.add), beside[1])
                V.tensor_copy(used[:, :], ranks[:, :, TB - 1])
                lk(V.tensor_tensor(slots[:, :, :], within, ranks[:, :, :], ALU.add), beside[2])
                lk(V.tensor_tensor(slots[:, :, :], slots[:, :, :], pairs[:, :, :], ALU.mult), beside[3])
                lk(V.tensor_reduce(slotf, over(slots), AXX, ALU.add))
                if not buf:
                    after(dve, scattered, 16 * TB * n)
                V.tensor_copy(tok[:, buf, :], tokf[:, :])
                V.tensor_copy(slot[:, buf, :], slotf).then_inc(slot_ready, 1)

            def step1(i, k, last=False):
                later = later_than_first(i)
                if later and k == 0:
                    if isinstance(i, int) and i == 1:
                        scales()
                    choose(i - 1, beside=tiles_of(i, 1) + tiles_of(i, 2) + tiles_of(i, 3))
                following = NONE if last else tiles_of(i + 1, 0)
                if k == 1:
                    if later and not (isinstance(i, int) and i == 1):
                        scale_of(i)
                    if not later:
                        for tile in tiles_of(i, 1) + tiles_of(i, 2) + tiles_of(i, 3):
                            tile()
                    deviations(i)
                if later and k == 2:
                    place(i - 1, beside=following)
                if k == 3:
                    if later:
                        weigh(i - 1, beside=newton_steps(i))
                    else:
                        for step in following + newton_steps(i):
                            step()
                    if isinstance(i, int) and i == 1:
                        low_sums(0, wscale[:, 0])
                        low_sums(1, wscale[:, 1], 1)
                    elif later:
                        low_sums(i, wsc[:, 0])
            dve.wait_ge(sort_init, 1)
            dve.wait_ge(info_init, 1)
            for tile in tiles_of(0, 0):
                tile()
            rounds(dve, R, step1, head=2)
            choose(R - 1)
            place(R - 1, 1)
            weigh(R - 1)

            count, tiles, end = (tq[:, c] for c in range(3))
            dve.wait_ge(slot_ready, R)
            V.memset(tmul[:, 0], 1.0)
            V.memset(tcmp[:, :, NQ:NQ + 1], 0.0)
            link(V.tensor_tensor(count, used[:, :], region_c, ALU.subtract))
            link(V.tensor_scalar(tiles, count, 1.0 / P, (P - 1) / (2.0 * P), ALU.mult, ALU.add))
            link(V.tensor_scalar(tiles, tiles, 8388608.0, None, ALU.add))
            link(V.tensor_scalar(tiles, tiles, 8388608.0, None, ALU.subtract))
            link(V.tensor_tensor_scan(end, tmul[:, 0], tiles, 0.0, ALU.mult, ALU.add))
            link(V.tensor_tensor(end, end, tiles, ALU.subtract))
            V.tensor_tensor(count, row_c, end, ALU.subtract)
            link(V.tensor_tensor(tcmp[:, :, 0:NQ], tile_c.unsqueeze(2).broadcast_to([P, 2, NQ]),
                                 end.unsqueeze(1).broadcast_to([P, 2, NQ]), ALU.is_ge))
            link(V.tensor_tensor(tone[:, :, :], tcmp[:, :, 0:NQ], tcmp[:, :, 1:NQ + 1], ALU.subtract))
            for c, values in enumerate((first_c, second_c, count)):
                link(V.tensor_tensor(tmul[:, :, :], tone[:, :, :], values.unsqueeze(1).broadcast_to([P, 2, NQ]), ALU.mult))
                link(V.tensor_reduce(tval[:, c], tmul[:, :, :], AXX, ALU.add))
            V.tensor_tensor(trow[:, :], tval[:, 2], tile_c, ALU.add).then_inc(rows_ready, 1)
            for e in range(NE):
                low_differences(e)
            dve.wait_ge(exps_mm, 1)
            V.tensor_copy(tile_exp[:, :, :], psum[0:1, 1, 0:4 * P].rearrange("o (v t) -> o v t", v=2)).then_inc(tiles_ready, 1)
            dve.wait_ge(rows_loaded, 32)
            V.tensor_copy(tokTf[:, :, :], tokT[:, :, :]).then_inc(rows_float, 1)
            dve.wait_ge(rows_turned, 1)
            V.tensor_copy(tile_tok[:, :], psum[:, 0, 0:2 * P]).then_inc(tiles_ready, 1)

            def gidx_copy(i, k):
                V.tensor_copy(gidx[:, k:k + 1], tile_tok[:, bass.ds(i * U + k, 1)]).then_inc(gidx_ready, 1)

            def split(i, k):
                j, b = i * U + k, k % 2
                dve.wait_ge(ld_x2[k], 32 * (i + 1))
                V.tensor_tensor(raw2[:, b, 0:H], x2[:, k, 0:H], x2[:, k, H:E], ALU.add).then_inc(raw_ready, 1)
                V.tensor_tensor(uv2[:, b, H:E], x2[:, k, 0:H], x2[:, k, H:E], ALU.subtract)
                dve.wait_ge(raw_ready, j + 1)
                V.scalar_tensor_tensor(uv2[:, b, 0:Q], raw2[:, b, 0:Q], inf2[:, k, 0:1], raw2[:, b, Q:H], ALU.subtract, ALU.add)
                V.tensor_tensor(uv2[:, b, Q:H], raw2[:, b, 0:Q], raw2[:, b, Q:H], ALU.subtract).then_inc(uv_ready, 1)
                dve.wait_ge(uv_ready, j + 1)
                after(dve, uvT_done, j - 1)
                V.tensor_scalar(hi2[:, b], uv2[:, b], inf2[:, k, 1:2], None, ALU.mult).then_inc(hi_ready, 1)
                dve.wait_ge(hi_ready, j + 1)
                V.scalar_tensor_tensor(lo2[:, b], uv2[:, b], inf2[:, k, 1:2], hi2[:, b], ALU.mult,
                                       ALU.subtract).then_inc(split_ready, 1)

            def step(i, k, last=False):
                j, b = i * U + k, k % 2
                dve.wait_ge(t_ready, j + 1)
                after(dve, g_ready, j - 1)
                dve.wait_ge(e_done, 2 * j + 2)
                V.scalar_tensor_tensor(z2[:, b], psum[:, 6 + b], inf2[:, k, 4:5], t2[:, b], ALU.mult,
                                       ALU.add).then_inc(z_ready, 1)
                if not (last and k + 2 >= U):
                    split(*at(i, k, 2))
                if not last:
                    gidx_copy(i + 1, k)
                if later_than_first(i):
                    dve.wait_ge(stored[b], 16 * ((i - 1) * (U // 2) + k // 2 + 1))
                dve.wait_ge(y_copied, j + 1)
                for part, sign in enumerate((ALU.add, ALU.subtract)):
                    ins = V.scalar_tensor_tensor(yp2[:, b, part * Q:(part + 1) * Q], psum[:, 2 + b, 0:Q], 1.0 / (XS * CS),
                                                 ysb2[:, b, Q:H], ALU.mult, sign)
                ins.then_inc(yp_ready, 1)
                dve.wait_ge(yp_ready, j + 1)
                for part, sign in enumerate((ALU.add, ALU.subtract)):
                    ins = V.tensor_tensor(s2[:, b, part * H:(part + 1) * H], yp2[:, b, 0:H], ysb2[:, b, H:E], sign)
                ins.then_inc(s_ready, 1)
                V.tensor_copy(sidx[:, k:k + 1], tile_tok[:, bass.ds(j, 1)]).then_inc(sidx_ready, 1)
                after(dve, o_ready, j - 1)
                dve.wait_ge(g_ready, j + 1)
                dve.wait_ge(s_ready, j + 1)
                V.tensor_tensor(sg2[:, b], s2[:, b], g2[:, b], ALU.mult).then_inc(sg_ready, 1)
            dve.wait_ge(tiles_ready, 2)
            for k in range(U):
                gidx_copy(0, k)
            split(0, 0)
            split(0, 1)
            rounds(dve, NT // U, step)

        @block.tensor
        def _(pe):
            mm = nc.tensor.matmul
            pe.wait_ge(ident_ready, 2)
            pe.wait_ge(ld_router, 16)
            for c in range(C):
                last = nc.tensor.transpose(psum[:, 3, c * NE:(c + 1) * NE], rtr[:, c * P:(c + 1) * P], ident[0:NE, 0:NE])
            last.then_inc(rt_mm, 1)
            pe.wait_ge(filt_ready, 1)
            for s in range(2):
                for ih in range(CH):
                    for kc in range(CH):
                        last = nc.tensor.matmul(psum[:, s, ih * H:(ih + 1) * H], tabf[:, 2 * s + kc, ih * P:(ih + 1) * P],
                                                tab[:, 2 * s + kc], start=(kc == 0), stop=(kc == CH - 1))
                last.then_inc(c_mm, 1)
            pe.wait_ge(wel_ready, 1)
            for s in range(2):
                pe.wait_ge(c_copied, s + 1)
                for ih in range(CH):
                    m = 2 * s + ih
                    for kc in range(CH):
                        last = nc.tensor.matmul(psum[:, 2, m * GOLAY_N:(m + 1) * GOLAY_N], cf[:, s, kc, ih * P:(ih + 1) * P],
                                                welpm[:, 2 * s + kc], start=(kc == 0), stop=(kc == CH - 1))
            last.then_inc(m_mm, 1)

            pe.wait_ge(wcat_raw, 1)
            pe.wait_ge(ones_ready, 1)
            for c in range(C):
                last = nc.tensor.matmul(psum[:, 4, 0:NL], avg[:, :], wcat[:, c, 0:NL], start=(c == 0), stop=(c == C - 1))
            last.then_inc(wmean_mm, 1)

            pe.wait_ge(c_lo_ready, 2)
            pe.wait_ge(wcat_ready, 1)

            def turn(i, k, q):
                t = (i * U + k) * GT + q
                if q == 0:
                    pe.wait_ge(ld_x[k], 16 * (i + 1))
                after(pe, t1_copied, t - GT + 1)
                for c in range(C):
                    last = nc.tensor.transpose(psum[:, TURN[q], c * P:(c + 1) * P], xbuf[:, k, q, c * P:(c + 1) * P], ident[:, :])
                last.then_inc(t1_done, 1)

            def logits(i, k):
                g = i * U + k
                pe.wait_ge(t1_copied, GT * (g + 1))
                after(pe, latT_copied, g)
                for c in range(C):
                    last = mm(psum[:, 2], wcat[:, c], xT4[:, k % 2, c], start=(c == 0), stop=(c == C - 1))
                last.then_inc(mm1_done, 1)

            def turn_back(i, k):
                pe.wait_ge(latT_copied, i * U + k + 1)
                after(pe, lat_copied, i)
                pe.sem_inc(latT_seen, 1)
                for q in range(GT):
                    t = k * GT + q
                    last = nc.tensor.transpose(psum[:, 4, t * NL:(t + 1) * NL], latT[0:NL, k % 2, q * P:(q + 1) * P],
                                               ident[0:NL, 0:NL])
                last.then_inc(back_done, 1)

            def rank(n):
                pe.wait_ge(pairs_ready, n + 1)
                onehot = pairs.rearrange("p q t -> p (q t)")
                mm(psum[:, 6, 0:NQ * TB], nbefore[:, :], onehot, start=True, stop=True)
                mm(psum[:, 7, 0:NQ * TB], ones[:, :], onehot, start=True, stop=True).then_inc(rank_mm, 1)

            def step1(i, k, last=False):
                ahead = not (last and k + 1 >= U)
                nxt = at(i, k, 1)
                if ahead:
                    turn(*nxt, 0)
                    turn(*nxt, 1)
                logits(i, k)
                if later_than_first(i) and k == 2:
                    rank(i - 1)
                if ahead:
                    turn(*nxt, 2)
                    turn(*nxt, 3)
                turn_back(i, k)
            pe.wait_ge(sort_init, 1)
            for q in range(GT):
                turn(0, 0, q)
            rounds(pe, R, step1)
            rank(R - 1)

            pe.wait_ge(rows_ready, 1)
            pe.wait_ge(t1_copied, T)
            for c in range(2):
                for h in range(2):
                    last = mm(psum[0:1, 1, (2 * c + h) * P:(2 * c + h + 1) * P], tval[:, c, h:h + 1], ident[:, :],
                              start=True, stop=True)
            last.then_inc(exps_mm, 1)
            pe.wait_ge(rows_float, 1)
            for h in range(2):
                last = nc.tensor.transpose(psum[:, 0, h * P:(h + 1) * P], tokTf[:, h], ident[:, :])
            last.then_inc(rows_turned, 1)

            pe.wait_ge(tiles_ready, 2)
            pe.wait_ge(wsum_ready, NE)
            pe.wait_ge(wlo_ready, NE)

            def front(i, k):
                j, b = i * U + k, k % 2
                pe.wait_ge(split_ready, j + 1)
                after(pe, hl_ready, j)
                nc.tensor.transpose(psum[0:96, 1, 0:P // 2].bitcast(BF16), inf2[:, k, 16:64].bitcast(BF16), ident_b[:, :])
                turned = psum[:, 0].bitcast(F16).rearrange("p (v c n) -> p v c n", v=2, c=C)
                for v_, part in enumerate((hi2, lo2)):
                    for c in range(C):
                        last = nc.tensor.transpose(turned[:, v_, c], part[:, b, c * P:(c + 1) * P], ident_h[:, :])
                last.then_inc(uvT_done, 1)

            def step(i, k, last=False):
                j, b = i * U + k, k % 2
                which = [pe.value_load(tile_exp[0:1, c, bass.ds(j, 1)], min_val=0, max_val=NE - 1) for c in range(2)]
                hi, lo = hl2[:, b, 0], hl2[:, b, 1]

                def expert(c_, e):
                    ps = psum[:, 4 + 2 * c_ + b]
                    for c in range(C):
                        wh = w_hi[:, bass.ds(e, 1), c].rearrange("p o n -> p (o n)")
                        wl = w_lo[:, bass.ds(e, 1), c].rearrange("p o n -> p (o n)")
                        mm(ps, hi[:, c], wh, start=(c == 0), stop=False)
                        mm(ps, hi[:, c], wl, start=False, stop=False)
                        end = mm(ps, lo[:, c], wh, start=False, stop=(c == C - 1))
                    end.then_inc(e_done, 1)
                after(pe, t_ready, j - 1)
                pe.wait_ge(hl_ready, j + 1)
                expert(0, which[0])
                if not (last and k + 1 >= U):
                    front(*at(i, k, 1))
                after(pe, z_ready, j - 1)
                expert(1, which[1])
                after(pe, s_ready, j - 1)
                yb = psum[:, 2 + b]
                mm(yb, bT2[:, b], wle3[:, :], start=True, stop=False)
                for c in range(C):
                    if c < 2:
                        ys, fh, fl = yb[:, c * Q:(c + 1) * Q], cq_hi[:, c], cq_lo[:, c]
                    else:
                        ys, fh, fl = yb[:, H:E], c_hi[:, c - 2], c_lo[:, c - 2]
                    mm(ys, hi[:, c], fh, start=False, stop=False)
                    mm(ys, hi[:, c], fl, start=False, stop=False)
                    end = mm(ys, lo[:, c], fh, start=False, stop=(c == C - 1))
                end.then_inc(y_done, 1)
            front(0, 0)
            rounds(pe, NT // U, step)


_INS = ["L0_attn_x", "L0_attn_W_el", "L0_attn_b_el", "L0_attn_W_le", "L0_attn_b_le", "L0_ffn_router_w",
        "L0_ffn_expert_weights"]


def kernel(**inputs):
    import concourse.bacc as bacc
    from concourse.bass_utils import run_bass_kernel_spmd as run

    nc = bacc.Bacc("TRN2", target_bir_lowering=False, num_devices=1)
    arrays, args = {}, []
    for name in _INS:
        a = np.ascontiguousarray(inputs[name])
        arrays[f"in_{name}"] = a
        args.append(nc.dram_tensor(f"in_{name}", a.shape, mybir.dt.from_np(a.dtype), kind="ExternalInput").ap())
    shape = arrays["in_L0_attn_x"].shape
    experts = arrays["in_L0_ffn_expert_weights"].shape[0]
    table = np.ascontiguousarray(np.concatenate([fourier_constants(shape[-1]), routing_constants(
        experts, shape[0] * shape[1], U * GT)], axis=1), dtype=np.float32)
    arrays["in_consts"] = table
    args.append(nc.dram_tensor("in_consts", table.shape, F32, kind="ExternalInput").ap())
    args.append(nc.dram_tensor("out_0", shape, F32, kind="ExternalOutput").ap())
    build(nc, *args)
    r = run(nc, [arrays], core_ids=[0])
    return r.results[0]["out_0"]
```
